# Optimizing a Trainium2 kernel written in Bass

```python
import numpy as np
import jax
import jax.numpy as jnp

def _softmax(x, axis=-1):
    return jax.nn.softmax(x, axis=axis)

def _gelu(x):
    return jax.nn.gelu(x, approximate=True)

def _silu(x):
    return jax.nn.silu(x)

def _sigmoid(x):
    return jax.nn.sigmoid(x)

def _layernorm(x, axis=-1, eps=1e-05):
    m = jnp.mean(x, axis=axis, keepdims=True)
    v = jnp.var(x, axis=axis, keepdims=True)
    return (x - m) / jnp.sqrt(v + eps)

def _scatter_add(tgt, idx, src, axis=0):
    return tgt.at[idx].add(src)

def _segment_sum(src, seg, n):
    return jax.ops.segment_sum(src, seg, n)
kernel_name = 'mk_adj_ffn_d1_adj_r2_495cfe'

def setup_inputs(seed: int=0):
    np.random.seed(seed)
    _w = jnp.asarray

    def _rec_inputs():
        import jax
        import jax.numpy as jnp
        _gk = jax.random.key(seed)
        x = 4.136e-05 + 0.9999 * jax.random.normal(jax.random.fold_in(_gk, 1), (2048, 256), jnp.float32)
        _a = jax.random.bernoulli(jax.random.fold_in(_gk, 2), 0.00195312, (2048, 2048))
        _a = jnp.logical_or(_a, jnp.swapaxes(_a, -1, -2))
        _af = _a.astype(jnp.float32)
        adj = _af
        return (x, adj)
    x, adj = _rec_inputs()

    def _L0_gnn_setup():
        import jax, jax.numpy as jnp
        import numpy as np
        N = 8192
        D_IN = 256
        D_OUT = 256
        AVG_DEG = 32.0
        key = jax.random.key(seed)
        k1, k2, k3, k4 = jax.random.split(key, 4)
        p = AVG_DEG / N
        adjacency = (jax.random.uniform(k1, (N, N)) < p).astype(jnp.float32)
        adjacency = jnp.maximum(adjacency, adjacency.T)
        node_degree = jnp.sum(adjacency, axis=1, keepdims=True) + 1.0
        x = jax.random.normal(k2, (N, D_IN), dtype=jnp.float32)
        W = jax.random.normal(k3, (D_IN, D_OUT), dtype=jnp.float32) * (1.0 / np.sqrt(D_IN))
        b = jax.random.normal(k4, (D_OUT,), dtype=jnp.float32) * 0.01
        return {'x': x, 'adjacency': adjacency, 'node_degree': node_degree, 'W': W, 'b': b}
    _L0_gnn_all = _L0_gnn_setup()
    _L0_gnn_in = {k: v for k, v in _L0_gnn_all.items() if k in ('W', 'b')}
    del _L0_gnn_all

    def _L0_ffn_setup():
        import jax, jax.numpy as jnp
        import numpy as np
        E = 8
        K = 1
        D = 256
        I = 1024
        B, T = (2, 1024)
        key = jax.random.key(seed)
        ks = jax.random.split(key, 7)
        s = 0.02
        x = jax.random.normal(ks[0], (B, T, D), jnp.float32)
        gate_w = jax.random.normal(ks[1], (E, D), jnp.float32) * s
        w1 = jax.random.normal(ks[2], (E, I, D), jnp.float32) * s
        w2 = jax.random.normal(ks[3], (E, D, I), jnp.float32) * s
        w3 = jax.random.normal(ks[4], (E, I, D), jnp.float32) * s
        sw1 = jax.random.normal(ks[5], (I, D), jnp.float32) * s
        sw2 = jax.random.normal(ks[6], (D, I), jnp.float32) * s
        return {'x': x, 'gate_w': gate_w, 'w1': w1, 'w2': w2, 'w3': w3, 'sw1': sw1, 'sw2': sw2}
    _L0_ffn_all = _L0_ffn_setup()
    _L0_ffn_in = {k: v for k, v in _L0_ffn_all.items() if k in ('gate_w', 'w1', 'w2', 'w3', 'sw1', 'sw2')}
    del _L0_ffn_all
    return {'x': x, 'adj': adj, 'L0_gnn_W': _L0_gnn_in['W'], 'L0_gnn_b': _L0_gnn_in['b'], 'L0_ffn_gate_w': _L0_ffn_in['gate_w'], 'L0_ffn_w1': _L0_ffn_in['w1'], 'L0_ffn_w2': _L0_ffn_in['w2'], 'L0_ffn_w3': _L0_ffn_in['w3'], 'L0_ffn_sw1': _L0_ffn_in['sw1'], 'L0_ffn_sw2': _L0_ffn_in['sw2']}

def reference(x, adj, L0_gnn_W, L0_gnn_b, L0_ffn_gate_w, L0_ffn_w1, L0_ffn_w2, L0_ffn_w3, L0_ffn_sw1, L0_ffn_sw2):
    import jax
    import jax.numpy as jnp

    def _L0_gnn_ref(x, adjacency, node_degree, W, b):
        import jax, jax.numpy as jnp
        import numpy as np
        N = 8192
        D_IN = 256
        D_OUT = 256
        AVG_DEG = 32.0
        n = adjacency.shape[0]
        a_hat = adjacency + jnp.eye(n, dtype=adjacency.dtype)
        dinv = jax.lax.rsqrt(node_degree)
        a_norm = dinv * a_hat * dinv
        pooled = a_norm @ x + x
        return jax.nn.relu(pooled @ W + b)

    def _L0_ffn_ref(x, gate_w, w1, w2, w3, sw1, sw2):
        import jax, jax.numpy as jnp
        import numpy as np
        E = 8
        K = 1
        D = 256
        I = 1024
        B, T = (2, 1024)
        xf = x.reshape(-1, D)
        logits = xf @ gate_w.T
        wts, idx = jax.lax.top_k(logits, K)
        wts = jax.nn.softmax(wts, axis=-1)
        comb = jnp.einsum('nke,nk->ne', jax.nn.one_hot(idx, E, dtype=xf.dtype), wts)
        h = jax.nn.silu(jnp.einsum('nd,eid->nei', xf, w1)) * jnp.einsum('nd,eid->nei', xf, w3)
        y = jnp.einsum('nei,edi->nd', h * comb[:, :, None], w2)
        y = y + jax.nn.gelu(xf @ sw1.T, approximate=False) @ sw2.T
        return y.reshape(x.shape)
    deg = jnp.maximum((adj != 0).astype(jnp.float32).sum(-1), 1.0)
    x = x + _L0_gnn_ref(_layernorm(x, axis=-1), adj, deg[..., None], L0_gnn_W, L0_gnn_b)
    x = x + _L0_ffn_ref(_layernorm(x, axis=-1)[None], L0_ffn_gate_w, L0_ffn_w1, L0_ffn_w2, L0_ffn_w3, L0_ffn_sw1, L0_ffn_sw2)[0]
    return x

_drawn_inputs = setup_inputs


def setup_inputs(seed=0):
    import zlib

    import numpy as np

    out = dict(_drawn_inputs(seed))
    spreads = {}
    factors = {'L0_gnn_b': 8.0}
    for name, (base, spread) in spreads.items():
        noise = np.random.default_rng([zlib.crc32(name.encode()), seed]).standard_normal(out[name].shape)
        drawn = base * np.exp(spread * noise) if base else spread * noise
        out[name] = jnp.asarray(drawn.astype(out[name].dtype))
    for name, factor in factors.items():
        out[name] = (out[name] * factor).astype(out[name].dtype)
    return out
```

```python
from contextlib import ExitStack

import concourse.bass as bass
from concourse import mybir

F32 = mybir.dt.float32
F32R = mybir.dt.float32r
BF16 = mybir.dt.bfloat16
I32 = mybir.dt.int32
U32 = mybir.dt.uint32
ALU = mybir.AluOpType
ACT = mybir.ActivationFunctionType
AX_X = mybir.AxisListType.X

P = 128
BANK = 512
EPS = 1e-5


def gnn_moe(nc, x_in, adj_t, w_in, b_in, gate_t, experts, sw1_t, sw2_t, out):
    N, D = x_in.shape
    E = gate_t.shape[1]
    I = sw1_t.shape[1]
    NT = N // P
    KD = D // P
    NI = I // P
    QT = BANK // P
    NQ = NT // QT
    CJ = 2
    NC = NT // CJ
    RAW = 4
    HALF = 2 * P
    NB = 2 * NQ * NI
    STEPS = NT + E - 1
    WCOL = experts.shape[2]
    W2AT = 2 * KD * I
    EC = 8
    ECW = WCOL // EC
    IH = I // BANK
    assert KD == 2 and IH == 2 and NT == NQ * QT and RAW % 2 == 0 and NC % RAW == 0

    sorted_x = nc.dram_tensor("sorted_x", (STEPS * P, D), F32, kind="Internal").ap()
    sorted_y = nc.dram_tensor("sorted_y", (STEPS * P, D), F32, kind="Internal").ap()

    base = (nc.sbuf_base + 31) // 32 * 32
    top = [base]
    size = {F32: 4, F32R: 4, BF16: 2, I32: 4, U32: 4}

    def place(name, shape, dtype, at=None):
        n = size[dtype]
        for k in shape[1:]:
            n *= k
        n = (n + 31) // 32 * 32
        where = top if at is None else at
        t = nc.alloc_sbuf_tensor_at(name, shape, dtype, offset=where[0])
        where[0] += n
        assert where[0] <= nc.sbuf_usable_end, (name, where[0])
        return t

    resid = place("resid", [P, NT, D], F32)
    norm = place("norm", [P, NT, D], F32)
    xfT_hi = place("xfT_hi", [P, 2, KD, BANK], F32R)
    xfT_lo = place("xfT_lo", [P, 2, KD, BANK], F32R)
    gel = place("gel", [P, 2, HALF], F32)
    gel_hi = place("gel_hi", [P, 2, HALF], F32R)
    gel_lo = place("gel_lo", [P, 2, HALF], F32R)
    xs = place("xs", [P, 2, D], F32)
    xsT_hi = place("xsT_hi", [P, KD, P], F32R)
    xsT_lo = place("xsT_lo", [P, KD, P], F32R)
    ident = place("ident", [P, P], F32)
    ident_r = place("ident_r", [P, P], F32R)
    ones = place("ones", [P, P], BF16)
    before = place("before", [P, P], BF16)
    gate_r = place("gate_r", [P, KD, HALF], F32R)
    gate_raw = place("gate_raw", [P, KD, E], F32)
    e_less = place("e_less", [P, NT, E], F32)
    k128 = place("k128", [P, E, NT], F32)
    s_iota = place("s_iota", [P, STEPS, E], F32)
    upto = place("upto", [P, E, E], F32)
    eps = place("eps", [P, 1], F32)
    stats = place("stats", [P, QT, 6], F32)
    mv = place("mv", [P, QT, 2], F32)
    rstd = place("rstd", [P, QT], F32)
    std = place("std", [P, QT], F32)
    deg = place("deg", [P, QT], F32)
    dinv2 = place("dinv2", [P, QT], F32)
    logit = place("logit", [P, NT, E], F32)
    top1 = place("top1", [P, NT], F32)
    choice = place("choice", [P, NT], F32)
    hot = place("hot", [P, NT, E], F32)
    hot_b = place("hot_b", [P, NT, E], BF16)
    rank = place("rank", [P, NT, E], F32)
    r_a = place("r_a", [P, NT, E], F32)
    scan = place("scan", [P, 2, NT // 2 + NT, E], F32)
    tiles = place("tiles", [P, E], F32)
    ends = place("ends", [P, E], F32)
    ebase = place("ebase", [P, E], F32)
    r_e = place("r_e", [P, E, NT], F32)
    r_s = place("r_s", [P, STEPS, E], F32)
    pos_f = place("pos_f", [P, NT], F32)
    pos = place("pos", [P, NT], U32)
    step_f = place("step_f", [P, STEPS], F32)
    step_chunks = place("step_chunks", [P, STEPS], I32)
    step_i = place("step_i", [P, STEPS], I32)
    step_slot = place("step_slot", [P, STEPS], I32)
    end_i = place("end_i", [P, E], I32)
    wt_d = place("wt_d", [P, NT], F32)
    wt_e = place("wt_e", [P, NT], F32)
    wt_r = place("wt_r", [P, NT], F32)
    wt = place("wt", [P, NT], F32)
    sw_at = [top[0]]
    sw1_hi = place("sw1_hi", [P, KD, I], F32R)
    sw1_lo = place("sw1_lo", [P, KD, I], F32R)
    sw2_r = place("sw2_r", [P, NI, 2, D], F32R)
    sil = place("sil", [P, I], F32, sw_at)
    hid = place("hid", [P, I], F32, sw_at)
    hidT_hi = place("hidT_hi", [P, NI, P], F32R, sw_at)
    hidT_lo = place("hidT_lo", [P, NI, P], F32R, sw_at)
    ysb = place("ysb", [P, 2, D], F32, sw_at)
    assert sw_at[0] <= top[0]
    zero_at = [top[0]]
    eraw = place("eraw", [P, 2, ECW], F32)
    zeros = place("zeros", [P, D], F32, zero_at)
    front = [top[0]]
    ering = place("ering", [P, 2, 2, WCOL], F32R)
    zz = place("zz", [P, NT, 2, D], F32R, front)
    araw = place("araw", [P, RAW, CJ, BANK], F32, front)
    a_hi = place("a_hi", [P, 2, CJ, BANK], F32R, front)
    a_lo = place("a_lo", [P, 2, CJ, BANK], F32R, front)
    sw1_raw = place("sw1_raw", [P, KD, I], F32, front)
    sw2_raw = place("sw2_raw", [P, NI, D], F32, front)
    w_raw = place("w_raw", [P, KD, D], F32, front)
    w_hi = place("w_hi", [P, KD, D], F32R, front)
    w_lo = place("w_lo", [P, KD, D], F32R, front)
    bias = place("bias", [P, D], F32, front)
    agg_at = [front[0]]
    xnT_hi = place("xnT_hi", [P, 2, KD, P], F32R, front)
    xnT_lo = place("xnT_lo", [P, 2, KD, P], F32R, front)
    agg = place("agg", [P, QT, D], F32, agg_at)
    count = place("count", [P, 2, CJ, BANK], BF16, front)
    assert front[0] <= top[0], (front[0], top[0])

    with ExitStack() as ctx:
        bank = [ctx.enter_context(nc.psum_tensor(f"bank{i}", [P, BANK], F32)) for i in range(8)]

        def sem(name):
            return ctx.enter_context(nc.semaphore(name))

        x_loaded = [sem(f"x_loaded{g}") for g in range(NQ)]
        bias_loaded = sem("bias_loaded")
        w_loaded = sem("w_loaded")
        shared_loaded = sem("shared_loaded")
        gate_loaded = sem("gate_loaded")
        adj_loaded = [sem(f"adj_loaded{r}") for r in range(RAW)]
        pad_zeroed = sem("pad_zeroed")
        consts = sem("consts")
        pool_self = sem("pool_self")
        dve_consts = sem("dve_consts")
        split_hi = sem("split_hi")
        split_lo = sem("split_lo")
        dve_self = sem("dve_self")
        act_self = sem("act_self")
        var_ready = sem("var_ready")
        std_ready = sem("std_ready")
        ln_ready = sem("ln_ready")
        xnT_ps = sem("xnT_ps")
        xnT_hi_ok = sem("xnT_hi_ok")
        xnT_lo_ok = sem("xnT_lo_ok")
        z_ps = sem("z_ps")
        z_hi_ok = sem("z_hi_ok")
        z_ok = sem("z_ok")
        adj_hi_ok = sem("adj_hi_ok")
        adj_lo_ok = sem("adj_lo_ok")
        adj_counted = sem("adj_counted")
        agg_chunk = sem("agg_chunk")
        agg_sum = sem("agg_sum")
        deg_ps = sem("deg_ps")
        dinv_ok = sem("dinv_ok")
        agg_scaled = sem("agg_scaled")
        agg_free = sem("agg_free")
        xfT_ps = sem("xfT_ps")
        xfT_hi_ok = sem("xfT_hi_ok")
        xfT_lo_ok = sem("xfT_lo_ok")
        logit_ps = sem("logit_ps")
        logit_ok = sem("logit_ok")
        sh_ps = sem("sh_ps")
        sh_gelu = sem("sh_gelu")
        sh_hi = sem("sh_hi")
        sh_lo = sem("sh_lo")
        sh_used = sem("sh_used")
        sh_free = sem("sh_free")
        hot_ok = sem("hot_ok")
        rank_ps = sem("rank_ps")
        rank_read = sem("rank_read")
        elo0_ok = sem("elo0_ok")
        routed = sem("routed")
        top1_ok = sem("top1_ok")
        exp_ok = sem("exp_ok")
        wt_ok = sem("wt_ok")
        scattered = sem("scattered")
        ehi_loaded = [sem(f"ehi_loaded{s}") for s in range(2)]
        eraw_loaded = [sem(f"eraw_loaded{s}") for s in range(2)]
        elo_ok = sem("elo_ok")
        xs_loaded = [sem(f"xs_loaded{s}") for s in range(2)]
        xsT_ps = sem("xsT_ps")
        xsT_hi_ok = sem("xsT_hi_ok")
        xsT_lo_ok = sem("xsT_lo_ok")
        up_ps = sem("up_ps")
        silu_ok = sem("silu_ok")
        hid_ok = sem("hid_ok")
        hidT_ps = sem("hidT_ps")
        hidT_hi_ok = sem("hidT_hi_ok")
        hidT_lo_ok = sem("hidT_lo_ok")
        steps_done = sem("steps_done")
        y_copied = sem("y_copied")
        y_ok = sem("y_ok")
        y_stored = [sem(f"y_stored{s}") for s in range(2)]
        gathered = [sem(f"gathered{q}") for q in range(NQ)]
        out_ok = sem("out_ok")
        out_stored = sem("out_stored")

        def acc(it):
            return bank[it]

        block = ctx.enter_context(nc.Block())

        @block.sync
        def _(sp):
            for g in range(NQ):
                sp.dma_start(resid[:, g * QT:(g + 1) * QT, :],
                             x_in[g * QT * P:(g + 1) * QT * P, :].rearrange("(t p) d -> p t d", p=P)
                             ).then_inc(x_loaded[g], 16)

            def chunk(q, c, n):
                if n is not None:
                    sp.wait_ge(adj_lo_ok, n - RAW + 1)
                    sp.wait_ge(adj_counted, n - RAW + 1)
                src = adj_t[c * CJ * P:(c + 1) * CJ * P, bass.ds(q * BANK, BANK)]
                sp.dma_start(araw[:, c % RAW, :, :], src.rearrange("(j p) i -> p j i", p=P)
                             ).then_inc(adj_loaded[c % RAW], 16)

            for c in range(NC):
                chunk(0, c, c if c >= RAW else None)
            with sp.Fori(1, NQ) as q:
                for c in range(NC):
                    chunk(q, c, q * NC + c)
            sp.wait_ge(pad_zeroed, 16)
            for e in range(E):
                for c in range(EC):
                    n = e * EC + c
                    if 2 <= n < EC + 2:
                        sp.wait_ge(elo0_ok, n - 1)
                    elif n >= 2:
                        sp.wait_ge(elo_ok, n - EC - 1)
                    sp.dma_start(eraw[:, c % 2, :], experts[e, :, c * ECW:(c + 1) * ECW]
                                 ).then_inc(eraw_loaded[c % 2], 16)
            for q in range(NQ):
                sp.wait_ge(out_ok, QT * (q + 1))
                sp.dma_start(out[q * QT * P:(q + 1) * QT * P, :].rearrange("(t p) d -> p t d", p=P),
                             resid[:, q * QT:(q + 1) * QT, :]).then_inc(out_stored, 16)
            sp.wait_ge(out_stored, 16 * NQ)

        @block.gpsimd
        def _(pool):
            selfs = [0]

            def then_wait(ins):
                selfs[0] += 1
                ins.then_inc(pool_self, 1)
                pool.wait_ge(pool_self, selfs[0])

            then_wait(pool.memset(ident[:], 0.0))
            pool.affine_select(out=ident[:], in_=ident[:], compare_op=ALU.not_equal, fill=1.0, base=0,
                               pattern=[[-1, P]], channel_multiplier=1).then_inc(consts, 1)
            pool.memset(zeros[:], 0.0).then_inc(consts, 1)
            then_wait(pool.memset(ones[:], 1.0))
            pool.affine_select(out=before[:], in_=ones[:], compare_op=ALU.is_gt, fill=0.0, base=0,
                               pattern=[[1, P]], channel_multiplier=-1).then_inc(consts, 1)
            then_wait(pool.memset(upto[:], 1.0))
            pool.affine_select(out=upto[:], in_=upto[:], compare_op=ALU.is_ge, fill=0.0, base=0,
                               pattern=[[1, E], [-1, E]], channel_multiplier=0).then_inc(consts, 1)
            pool.iota(e_less[:], pattern=[[0, NT], [1, E]], base=-E, channel_multiplier=0,
                      allow_small_or_imprecise_dtypes=True).then_inc(consts, 1)
            pool.iota(k128[:], pattern=[[0, E], [P, NT]], base=0, channel_multiplier=0,
                      allow_small_or_imprecise_dtypes=True).then_inc(consts, 1)
            pool.iota(s_iota[:], pattern=[[1, STEPS], [0, E]], base=0, channel_multiplier=0,
                      allow_small_or_imprecise_dtypes=True).then_inc(consts, 1)

            def adj_low(s, r, n):
                pool.wait_ge(adj_hi_ok, n)
                pool.tensor_tensor(a_lo[:, s, :, :], araw[:, r, :, :], a_hi[:, s, :, :].bitcast(F32),
                                   ALU.subtract).then_inc(adj_lo_ok, 1)

            def adj_lows(q):
                with pool.Fori(0, NC // RAW) as c:
                    for u in range(RAW):
                        adj_low(u % 2, u, q * NC + c * RAW + u + 1)

            def shared_lows(first, n):
                with pool.Fori(0, n // 2) as m:
                    for u in range(2):
                        pool.wait_ge(sh_hi, m * 2 + (first + u + 1))
                        pool.tensor_tensor(gel_lo[:, u, :], gel[:, u, :], gel_hi[:, u, :].bitcast(F32),
                                           ALU.subtract).then_inc(sh_lo, 1)

            def expert_high(e, slot):
                pool.dma_start(ering[:, slot, 0, :], experts[bass.ds(e, 1), :, :].rearrange("a p n -> (a p) n")
                               ).then_inc(ehi_loaded[slot], 16)

            def expert_lows(e, slot, uses):
                pool.wait_ge(ehi_loaded[slot], uses * 16)
                for c in range(EC):
                    pool.wait_ge(eraw_loaded[c % 2], (e * (EC // 2) + (c // 2 + 1)) * 16)
                    pool.tensor_tensor(ering[:, slot, 1, c * ECW:(c + 1) * ECW], eraw[:, c % 2, :],
                                             ering[:, slot, 0, c * ECW:(c + 1) * ECW].bitcast(F32),
                                             ALU.subtract).then_inc(elo_ok, 1)

            for q in range(NQ):
                adj_lows(q)
                if q:
                    shared_lows((q - 1) * 2 * NI, 2 * NI if q < NQ - 1 else NI)
            pool.wait_ge(agg_free, NT)
            for e in range(2):
                expert_high(e, e)
            shared_lows((2 * NQ - 3) * NI, 2 * NI)
            pool.wait_ge(pad_zeroed, 16)
            pool.wait_ge(routed, 2)
            for t in range(NT):
                pool.indirect_dma_start(out=sorted_x, out_offset=bass.IndirectOffsetOnAxis(ap=pos[:, t:t + 1], axis=0),
                                        in_=norm[:, t, :], in_offset=None).then_inc(scattered, 16)
            expert_lows(1, 1, 1)
            with pool.Fori(1, E // 2) as pair:
                for u in range(2):
                    last = pool.value_load(end_i[0:1, bass.ds(pair * 2 + (u - 2), 1)], min_val=1, max_val=STEPS + 1)
                    pool.wait_ge(steps_done, last)
                    expert_high(pair * 2 + u, u)
                    expert_lows(pair * 2 + u, u, pair + 1)
            for s in range(2):
                pool.wait_ge(y_stored[s], 16 * ((STEPS + 1 - s) // 2))
            for t in range(NT):
                pool.indirect_dma_start(out=norm[:, t, :], out_offset=None, in_=sorted_y,
                                        in_offset=bass.IndirectOffsetOnAxis(ap=pos[:, t:t + 1], axis=0)
                                        ).then_inc(gathered[t // QT], 16)

        @block.scalar
        def _(act):
            act.dma_start(bias[:], b_in.rearrange("(a d) -> a d", a=1).partition_broadcast(P)
                          ).then_inc(bias_loaded, 16)
            act.dma_start(w_raw[:], w_in.rearrange("(k p) n -> p k n", p=P)).then_inc(w_loaded, 16)
            act.dma_start(gate_raw[:], gate_t.rearrange("(k p) n -> p k n", p=P)).then_inc(gate_loaded, 16)
            act.dma_start(sw1_raw[:], sw1_t.rearrange("(k p) n -> p k n", p=P)).then_inc(shared_loaded, 16)
            act.dma_start(sw2_raw[:], sw2_t.rearrange("(k p) n -> p k n", p=P)).then_inc(shared_loaded, 16)
            act.wait_ge(consts, 2)
            act.dma_start(sorted_x.rearrange("(s p) d -> p s d", p=P),
                          zeros[:, :].rearrange("p (a d) -> p a d", a=1).to_broadcast([P, STEPS, D])
                          ).then_inc(pad_zeroed, 16)

            act.activation(ident_r[:], ident[:], ACT.Copy).then_inc(split_hi, 1)
            act.wait_ge(w_loaded, 16)
            act.activation(w_hi[:], w_raw[:], ACT.Copy).then_inc(split_hi, 1)

            def stds(k):
                act.wait_ge(var_ready, QT * (k + 1))
                act.activation(std[:], mv[:, :, 1], ACT.Sqrt, bias=eps[:, 0:1]).then_inc(std_ready, 1)

            def z_tile(t):
                act.wait_ge(xnT_ps, t + 1)
                if t >= 2:
                    act.wait_ge(z_ps, t - 1)
                act.activation(xnT_hi[:, t % 2], bank[4 + t % 2][:, 0:D].rearrange("p (k n) -> p k n", k=KD),
                               ACT.Copy).then_inc(xnT_hi_ok, 1)
                act.wait_ge(z_ps, t + 1)
                act.activation(zz[:, t, 0, :], bank[6 + t % 2][:, 0:D], ACT.Copy).then_inc(z_hi_ok, 1)

            def adj_high(s, r, loads, n):
                act.wait_ge(adj_loaded[r], loads * 16)
                if n is not None:
                    act.wait_ge(agg_chunk, n)
                act.activation(a_hi[:, s, :, :], araw[:, r, :, :], ACT.Copy).then_inc(adj_hi_ok, 1)

            act.wait_ge(dve_consts, 2)
            stds(0)
            for t in range(NT):
                z_tile(t)
                if t % QT == 0 and t // QT + 1 < NQ:
                    stds(t // QT + 1)
                if t % CJ == CJ - 1:
                    c = t // CJ
                    adj_high(c % 2, c % RAW, c // RAW + 1, c - 1 if c >= 2 else None)
                if t == 3:
                    act.wait_ge(gate_loaded, 16)
                    act.activation(gate_r[:, :, 0:E], gate_raw[:], ACT.Copy).then_inc(split_hi, 1)
                    act.wait_ge(shared_loaded, 32)
                    act.activation(sw1_hi[:], sw1_raw[:], ACT.Copy).then_inc(split_hi, 1)
                    act.activation(sw2_r[:, :, 0, :], sw2_raw[:], ACT.Copy).then_inc(split_hi, 1)

            def adj_highs(q):
                with act.Fori(0, NC // RAW) as c:
                    for u in range(RAW):
                        adj_high(u % 2, u, c + (q * NC // RAW + 1), q * NC + c * RAW + (u - 1))

            def scale_sums(q):
                act.wait_ge(agg_sum, q + 1)
                act.wait_ge(dinv_ok, q + 1)
                for it in range(QT):
                    act.activation(agg[:, it, :], acc(it)[:, 0:D], ACT.Copy, scale=dinv2[:, it:it + 1]
                                   ).then_inc(agg_scaled, 1)

            def xfT_highs(q):
                for it in range(QT):
                    t = q * QT + it
                    act.wait_ge(xfT_ps, t + 1)
                    act.activation(xfT_hi[:, q % 2, :, it * P:(it + 1) * P],
                                   bank[4 + t % 2][:, 0:D].rearrange("p (k n) -> p k n", k=KD),
                                   ACT.Copy).then_inc(xfT_hi_ok, 1)

            def shared_blocks(first, n):
                def one(u, m, early):
                    act.wait_ge(sh_ps, m + 1)
                    if not early:
                        act.wait_ge(sh_lo, m - 1)
                    act.activation(gel[:, u, :], bank[4 + u][:, 0:HALF], ACT.Gelu).then_inc(sh_gelu, 1)
                    act.wait_ge(sh_gelu, m + 1)
                    if not early:
                        act.wait_ge(sh_used, m - 1)
                    act.activation(gel_hi[:, u, :], gel[:, u, :], ACT.Copy).then_inc(sh_hi, 1)

                skip = 2 if first == 0 else 0
                for m in range(skip):
                    one(m, m, True)
                with act.Fori(0, (n - skip) // 2) as m:
                    for u in range(2):
                        one(u, m * 2 + (first + skip + u), False)

            scale_sums(0)
            for q in range(1, NQ):
                adj_highs(q)
                stds(NQ + q - 1)
                xfT_highs(q - 1)
                scale_sums(q)
                shared_blocks((q - 1) * 2 * NI, 2 * NI if q < NQ - 1 else NI)
            stds(2 * NQ - 1)
            xfT_highs(NQ - 1)
            shared_blocks((2 * NQ - 3) * NI, 3 * NI)
            act.wait_ge(top1_ok, 1)
            act.activation(wt_e[:], wt_d[:], ACT.Exp).then_inc(exp_ok, 1)

            def load_rows(s, u, dep):
                if dep is not None:
                    act.wait_ge(xsT_ps, dep)
                act.dma_start(xs[:, u, :], sorted_x[bass.ds(s * P, P), :]).then_inc(xs_loaded[u], 16)

            def rows_high(n):
                act.wait_ge(xsT_ps, n)
                act.activation(xsT_hi[:], bank[7][:, 0:D].rearrange("p (k n) -> p k n", k=KD), ACT.Copy
                               ).then_inc(xsT_hi_ok, 1)

            def silus(s):
                for h in range(IH):
                    act.wait_ge(up_ps, s * IH + (h + 1))
                    act.activation(sil[:, h * BANK:(h + 1) * BANK], bank[h][:, :], ACT.Silu).then_inc(silu_ok, 1)

            def y_copy(s, u, reuse):
                act.wait_ge(steps_done, s + 2)
                if reuse is not None:
                    act.wait_ge(y_stored[u], reuse * 16)
                act.activation(ysb[:, u, :], bank[6][:, 0:D], ACT.Copy).then_inc(y_copied, 1)

            def hid_highs(s):
                for h in range(IH):
                    act.wait_ge(hidT_ps, s * IH + (h + 1))
                    act.activation(hidT_hi[:, h * 4:(h + 1) * 4, :],
                                   bank[4 + h][:, :].rearrange("p (k n) -> p k n", n=P), ACT.Copy
                                   ).then_inc(hidT_hi_ok, 1)

            def y_store(s, u):
                act.wait_ge(y_ok, s + 1)
                act.dma_start(sorted_y[bass.ds(s * P, P), :], ysb[:, u, :]).then_inc(y_stored[u], 16)

            def step(s, u, i):
                if not isinstance(s, int) or s + 2 < STEPS:
                    load_rows(s + 2, 1 - u, s + 1)
                silus(s)
                if not isinstance(s, int) or s + 1 < STEPS:
                    rows_high(s + 2)
                y_copy(s - 1, u, None if isinstance(i, int) and i == 0 else i)
                hid_highs(s)
                y_store(s - 1, u)

            act.wait_ge(scattered, 16 * NT)
            load_rows(0, 0, None)
            load_rows(1, 1, None)
            rows_high(1)
            load_rows(2, 0, 1)
            silus(0)
            rows_high(2)
            hid_highs(0)
            for u in range(2):
                step(1 + u, u, 0)
            with act.Fori(1, (STEPS - 3) // 2) as i:
                for u in range(2):
                    step(i * 2 + (1 + u), u, i)
            for u in range(2):
                step(STEPS - 2 + u, u, (STEPS - 3) // 2)
            y_copy(STEPS - 1, 0, (STEPS - 1) // 2)
            y_store(STEPS - 1, 0)

        @block.vector
        def _(dve):
            selfs = [0]

            def chained(ins):
                selfs[0] += 1
                ins.then_inc(dve_self, 1)

            def settle():
                dve.wait_ge(dve_self, selfs[0])

            dve.memset(eps[:], EPS).then_inc(dve_consts, 1)
            dve.memset(gate_r[:].bitcast(F32), 0.0).then_inc(dve_consts, 1)
            chained(dve.memset(scan[:], 0.0))

            def variances(k, tiles_of):
                for i, t in enumerate(tiles_of):
                    chained(dve.bn_stats(stats[:, i, :], resid[:, t, :]))
                settle()
                for i, t in enumerate(tiles_of):
                    dve.bn_aggr(mv[:, i, :], stats[:, i, :]).then_inc(var_ready, 1)

            def normalize(k, tiles_of):
                dve.wait_ge(std_ready, k + 1)
                chained(dve.reciprocal(rstd[:], std[:]))
                settle()
                for i, t in enumerate(tiles_of):
                    dve.tensor_scalar(norm[:, t, :], resid[:, t, :], mv[:, i, 0:1], rstd[:, i:i + 1],
                                      ALU.subtract, ALU.mult).then_inc(ln_ready, 1)

            def group(q):
                return range(q * QT, (q + 1) * QT)

            def z_tile(t):
                dve.wait_ge(xnT_hi_ok, t + 1)
                dve.tensor_tensor(xnT_lo[:, t % 2], bank[4 + t % 2][:, 0:D].rearrange("p (k n) -> p k n", k=KD),
                                  xnT_hi[:, t % 2].bitcast(F32), ALU.subtract).then_inc(xnT_lo_ok, 1)
                dve.wait_ge(z_hi_ok, t + 1)
                dve.tensor_tensor(zz[:, t, 1, :], bank[6 + t % 2][:, 0:D], zz[:, t, 0, :].bitcast(F32),
                                  ALU.subtract).then_inc(z_ok, 1)
                dve.tensor_tensor(norm[:, t, :], bank[6 + t % 2][:, 0:D], bias[:], ALU.add).then_inc(z_ok, 1)

            def count_chunk(q, r, loads, n, first):
                dve.wait_ge(adj_loaded[r], loads * 16)
                into = count[:, q % 2, :, :]
                if first:
                    dve.tensor_scalar(into, araw[:, r, :, :], 0.0, None, ALU.not_equal).then_inc(adj_counted, 1)
                else:
                    dve.wait_ge(adj_counted, n)
                    dve.scalar_tensor_tensor(into, araw[:, r, :, :], 0.0, into, ALU.not_equal, ALU.add
                                             ).then_inc(adj_counted, 1)

            dve.wait_ge(x_loaded[0], 16)
            variances(0, group(0))
            normalize(0, group(0))
            dve.wait_ge(w_loaded, 16)
            dve.wait_ge(split_hi, 2)
            dve.tensor_tensor(w_lo[:], w_raw[:], w_hi[:].bitcast(F32), ALU.subtract).then_inc(split_lo, 1)
            dve.wait_ge(bias_loaded, 16)
            for t in range(NT):
                if t % QT == 0 and t // QT + 1 < NQ:
                    g = t // QT + 1
                    dve.wait_ge(x_loaded[g], 16)
                    dve.wait_ge(ln_ready, g * QT)
                    variances(g, group(g))
                z_tile(t)
                if t % QT == 1 and t // QT + 1 < NQ:
                    normalize(t // QT + 1, group(t // QT + 1))
                if t % CJ == CJ - 1:
                    c = t // CJ
                    count_chunk(0, c % RAW, c // RAW + 1, c, c == 0)
                if t == 5:
                    dve.wait_ge(split_hi, 3)
                    dve.tensor_tensor(gate_r[:, :, E:2 * E], gate_raw[:], gate_r[:, :, 0:E].bitcast(F32),
                                      ALU.subtract).then_inc(split_lo, 1)
                    dve.wait_ge(split_hi, 5)
                    dve.tensor_tensor(sw1_lo[:], sw1_raw[:], sw1_hi[:].bitcast(F32), ALU.subtract
                                      ).then_inc(split_lo, 1)
                    dve.tensor_tensor(sw2_r[:, :, 1, :], sw2_raw[:], sw2_r[:, :, 0, :].bitcast(F32),
                                      ALU.subtract).then_inc(split_lo, 1)

            def count_chunks(q):
                count_chunk(q, 0, q * NC // RAW + 1, q * NC, True)
                for u in range(1, RAW):
                    count_chunk(q, u, q * NC // RAW + 1, q * NC + u, False)
                with dve.Fori(1, NC // RAW) as c:
                    for u in range(RAW):
                        count_chunk(q, u, c + (q * NC // RAW + 1), q * NC + c * RAW + u, False)

            def inverse_degree(q):
                dve.wait_ge(deg_ps, q + 1)
                chained(dve.tensor_scalar(deg[:], bank[4][:, 0:QT], 1.0, None, ALU.max))
                settle()
                dve.reciprocal(dinv2[:], deg[:]).then_inc(dinv_ok, 1)

            def finish_gnn(q):
                dve.wait_ge(dinv_ok, q + 1)
                for it in range(QT):
                    dve.wait_ge(agg_scaled, q * QT + it + 1)
                    dve.scalar_tensor_tensor(agg[:, it, :], acc(it)[:, D:2 * D], dinv2[:, it:it + 1],
                                             agg[:, it, :], ALU.mult, ALU.add).then_inc(agg_free, 1)
                dve.wait_ge(agg_free, (q + 1) * QT)
                for it, t in enumerate(group(q)):
                    chained(dve.tensor_tensor(agg[:, it, :], agg[:, it, :], norm[:, t, :], ALU.add))
                settle()
                for it, t in enumerate(group(q)):
                    chained(dve.scalar_tensor_tensor(resid[:, t, :], agg[:, it, :], 0.0, resid[:, t, :],
                                                     ALU.max, ALU.add))
                settle()

            def xfT_lows(q):
                for it in range(QT):
                    t = q * QT + it
                    dve.wait_ge(xfT_hi_ok, t + 1)
                    dve.tensor_tensor(xfT_lo[:, q % 2, :, it * P:(it + 1) * P],
                                      bank[4 + t % 2][:, 0:D].rearrange("p (k n) -> p k n", k=KD),
                                      xfT_hi[:, q % 2, :, it * P:(it + 1) * P].bitcast(F32),
                                      ALU.subtract).then_inc(xfT_lo_ok, 1)

            def logits(q):
                for t in group(q):
                    dve.wait_ge(logit_ps, t + 1)
                    chained(dve.tensor_copy(logit[:, t, :], bank[6 + t % 2][:, E:2 * E]))
                    settle()
                    dve.tensor_tensor(logit[:, t, :], bank[6 + t % 2][:, 0:E], logit[:, t, :], ALU.add
                                      ).then_inc(logit_ok, 1)

            def add_shared(hq):
                dve.wait_ge(sh_used, (hq + 1) * NI)
                for k in range(2):
                    chained(dve.tensor_tensor(resid[:, hq * 2 + k, :], bank[6 + k][:, 0:D],
                                              resid[:, hq * 2 + k, :], ALU.add))
                settle()
                for k in range(2):
                    dve.tensor_tensor(resid[:, hq * 2 + k, :], bank[6 + k][:, D:2 * D],
                                      resid[:, hq * 2 + k, :], ALU.add).then_inc(sh_free, 1)

            inverse_degree(0)
            finish_gnn(0)
            variances(NQ, group(0))
            for q in range(1, NQ):
                count_chunks(q)
                normalize(NQ + q - 1, group(q - 1))
                inverse_degree(q)
                xfT_lows(q - 1)
                logits(q - 1)
                finish_gnn(q)
                dve.wait_ge(ln_ready, NT + q * QT)
                variances(NQ + q, group(q))
                add_shared(2 * (q - 1))
                if q < NQ - 1:
                    add_shared(2 * (q - 1) + 1)
            normalize(2 * NQ - 1, group(NQ - 1))
            xfT_lows(NQ - 1)
            logits(NQ - 1)

            dve.wait_ge(logit_ok, NT)
            dve.wait_ge(consts, 7)

            def step(ins):
                chained(ins)
                settle()

            def over_e(ap):
                return ap.rearrange("p (t a) -> p t a", a=1).to_broadcast([P, NT, E])

            step(dve.tensor_reduce(top1[:], logit[:], AX_X, ALU.max))
            step(dve.tensor_tensor(hot[:], logit[:], over_e(top1[:]), ALU.is_equal))
            step(dve.tensor_tensor(r_a[:], hot[:], e_less[:], ALU.mult))
            step(dve.tensor_reduce(choice[:], r_a[:], AX_X, ALU.min))
            step(dve.tensor_tensor(hot[:], e_less[:], over_e(choice[:]), ALU.is_equal))
            dve.tensor_copy(hot_b[:], hot[:]).then_inc(hot_ok, 1)
            dve.tensor_tensor(wt_d[:], top1[:], top1[:], ALU.subtract).then_inc(top1_ok, 1)
            add_shared(2 * NQ - 3)
            dve.wait_ge(rank_ps, 1)
            ZT = NT // 2
            step(dve.tensor_copy(scan[:, 0, ZT:, :], bank[6][:, 0:NT * E].rearrange("p (t e) -> p t e", e=E)))
            step(dve.tensor_tensor(rank[:], bank[7][:, 0:NT * E].rearrange("p (t e) -> p t e", e=E),
                                   scan[:, 0, ZT:, :], ALU.subtract))
            dve.engine_nop().then_inc(rank_read, 1)
            a = 0
            for sh in (1, 2, 4, 8):
                step(dve.tensor_tensor(scan[:, 1 - a, ZT:, :], scan[:, a, ZT:, :],
                                       scan[:, a, ZT - sh:ZT - sh + NT, :], ALU.add))
                a = 1 - a
            total = scan[:, a, ZT + NT - 1, :]
            step(dve.tensor_tensor(r_e[:], total.rearrange("p (e a) -> p e a", a=1).to_broadcast([P, E, NT]),
                                   k128[:], ALU.is_gt))
            step(dve.tensor_reduce(tiles[:], r_e[:], AX_X, ALU.add))
            step(dve.tensor_tensor(r_e[:, :, 0:E],
                                   tiles[:].rearrange("p (a e) -> p a e", a=1).to_broadcast([P, E, E]),
                                   upto[:], ALU.mult))
            step(dve.tensor_reduce(ends[:], r_e[:, :, 0:E], AX_X, ALU.add))
            step(dve.tensor_tensor(ebase[:], ends[:], tiles[:], ALU.subtract))
            step(dve.tensor_tensor(r_a[:], scan[:, a, ZT:, :], rank[:], ALU.add))
            step(dve.tensor_scalar(ebase[:], ebase[:], float(P), None, ALU.mult))
            step(dve.tensor_tensor(r_a[:], r_a[:],
                                   ebase[:].rearrange("p (a e) -> p a e", a=1).to_broadcast([P, NT, E]), ALU.add))
            step(dve.tensor_tensor(r_a[:], r_a[:], hot[:], ALU.mult))
            step(dve.tensor_reduce(pos_f[:], r_a[:], AX_X, ALU.add))
            dve.tensor_copy(pos[:], pos_f[:]).then_inc(routed, 1)
            step(dve.tensor_tensor(r_s[:], ends[:].rearrange("p (a e) -> p a e", a=1).to_broadcast([P, STEPS, E]),
                                   s_iota[:], ALU.is_le))
            step(dve.tensor_reduce(step_f[:], r_s[:], AX_X, ALU.add))
            step(dve.tensor_scalar(step_i[:], step_f[:], float(E - 1), None, ALU.min))
            step(dve.tensor_scalar(step_slot[:], step_i[:], 1, None, ALU.bitwise_and))
            step(dve.tensor_scalar(step_f[:], step_f[:], float(E - 1), float(EC), ALU.min, ALU.mult))
            step(dve.tensor_scalar(step_chunks[:], step_f[:], 1.0, None, ALU.max))
            dve.tensor_scalar(end_i[:], ends[:], 1.0, None, ALU.add).then_inc(routed, 1)
            add_shared(2 * NQ - 2)
            for m in range(NB - NI, NB):
                dve.wait_ge(sh_hi, m + 1)
                dve.tensor_tensor(gel_lo[:, m % 2, :], gel[:, m % 2, :], gel_hi[:, m % 2, :].bitcast(F32),
                                  ALU.subtract).then_inc(sh_lo, 1)
            add_shared(2 * NQ - 1)
            dve.wait_ge(ehi_loaded[0], 16)
            for c in range(EC):
                dve.wait_ge(eraw_loaded[c % 2], (c // 2 + 1) * 16)
                dve.tensor_tensor(ering[:, 0, 1, c * ECW:(c + 1) * ECW], eraw[:, c % 2, :],
                                  ering[:, 0, 0, c * ECW:(c + 1) * ECW].bitcast(F32),
                                  ALU.subtract).then_inc(elo0_ok, 1)
            dve.wait_ge(exp_ok, 1)
            step(dve.reciprocal(wt_r[:], wt_e[:]))
            dve.tensor_tensor(wt[:], wt_e[:], wt_r[:], ALU.mult).then_inc(wt_ok, 1)

            def rows_low(n):
                dve.wait_ge(xsT_hi_ok, n)
                dve.tensor_tensor(xsT_lo[:], bank[7][:, 0:D].rearrange("p (k n) -> p k n", k=KD),
                                  xsT_hi[:].bitcast(F32), ALU.subtract).then_inc(xsT_lo_ok, 1)

            def hids(s):
                for h in range(IH):
                    dve.wait_ge(silu_ok, s * IH + (h + 1))
                    dve.tensor_tensor(hid[:, h * BANK:(h + 1) * BANK], bank[2 + h][:, :],
                                      sil[:, h * BANK:(h + 1) * BANK], ALU.mult).then_inc(hid_ok, 1)

            def hid_lows(s):
                for h in range(IH):
                    dve.wait_ge(hidT_hi_ok, s * IH + (h + 1))
                    dve.tensor_tensor(hidT_lo[:, h * 4:(h + 1) * 4, :],
                                      bank[4 + h][:, :].rearrange("p (k n) -> p k n", n=P),
                                      hidT_hi[:, h * 4:(h + 1) * 4, :].bitcast(F32), ALU.subtract
                                      ).then_inc(hidT_lo_ok, 1)

            def y_add(s, u):
                dve.wait_ge(y_copied, s + 1)
                dve.tensor_tensor(ysb[:, u, :], bank[6][:, D:2 * D], ysb[:, u, :], ALU.add).then_inc(y_ok, 1)

            rows_low(1)
            hids(0)
            rows_low(2)
            hid_lows(0)
            def one_step(s, u, more):
                hids(s)
                if more:
                    rows_low(s + 2)
                y_add(s - 1, u)
                hid_lows(s)

            with dve.Fori(0, (STEPS - 3) // 2) as i:
                for u in range(2):
                    one_step(i * 2 + (1 + u), u, True)
            for u in range(2):
                one_step(STEPS - 2 + u, u, u == 0)
            y_add(STEPS - 1, (STEPS - 1) % 2)
            dve.wait_ge(wt_ok, 1)
            for q in range(NQ):
                dve.wait_ge(gathered[q], 16 * QT)
                for t in group(q):
                    dve.scalar_tensor_tensor(resid[:, t, :], norm[:, t, :], wt[:, t:t + 1], resid[:, t, :],
                                             ALU.mult, ALU.add).then_inc(out_ok, 1)

        @block.tensor
        def _(pe):
            def transposes(into, source):
                for k in range(KD):
                    ins = pe.transpose(into[:, k * P:(k + 1) * P], source[:, k * P:(k + 1) * P], ident[:])
                return ins

            def xn_transpose(t):
                pe.wait_ge(ln_ready, t + 1)
                if t >= 2:
                    pe.wait_ge(xnT_lo_ok, t - 1)
                transposes(bank[4 + t % 2], norm[:, t, :]).then_inc(xnT_ps, 1)

            def z_tile(t):
                pe.wait_ge(xnT_lo_ok, t + 1)
                if t >= 2:
                    pe.wait_ge(z_ok, 2 * (t - 1))
                n = 0
                for k in range(KD):
                    for a, w in ((xnT_hi, w_hi), (xnT_lo, w_hi), (xnT_hi, w_lo)):
                        ins = pe.matmul(bank[6 + t % 2][:, 0:D], a[:, t % 2, k, :], w[:, k, :],
                                        start=n == 0, stop=n == 3 * KD - 1)
                        n += 1
                ins.then_inc(z_ps, 1)

            def agg_part(s, j, zt, first):
                for it in range(QT):
                    pe.matmul(acc(it)[:, :], a_hi[:, s, j, it * P:(it + 1) * P], zt,
                              start=first, stop=False)
                    ins = pe.matmul(acc(it)[:, 0:D], a_lo[:, s, j, it * P:(it + 1) * P], zt[:, 0:D],
                                    start=False, stop=False)
                return ins

            def z_of(t):
                return zz[:, bass.ds(t, 1), :, :].rearrange("p a h d -> p (a h d)")

            def agg_end(q):
                for it in range(QT):
                    ins = pe.matmul(acc(it)[:, :], ident_r[:], zz[:, q * QT + it, :, :].rearrange("p h d -> p (h d)"),
                                    start=False, stop=True)
                ins.then_inc(agg_sum, 1)
                pe.wait_ge(adj_counted, (q + 1) * NC)
                if q == 0:
                    pe.wait_ge(xnT_lo_ok, NT)
                for it in range(QT):
                    for j in range(CJ):
                        ins = pe.matmul(bank[4][:, it:it + 1], count[:, q % 2, j, it * P:(it + 1) * P],
                                        ones[:, 0:1], start=j == 0, stop=j == CJ - 1)
                ins.then_inc(deg_ps, 1)

            pe.wait_ge(consts, 3)
            pe.wait_ge(split_lo, 1)
            xn_transpose(0)
            for t in range(NT):
                if t + 1 < NT:
                    xn_transpose(t + 1)
                z_tile(t)
                if t % CJ == CJ - 1 and t // CJ >= 1:
                    c = t // CJ - 1
                    pe.wait_ge(z_ok, 2 * (c + 1) * CJ)
                    pe.wait_ge(adj_lo_ok, c + 1)
                    for j in range(CJ):
                        ins = agg_part(c % 2, j, z_of(c * CJ + j), c == 0 and j == 0)
                    ins.then_inc(agg_chunk, 1)
            c = NC - 1
            pe.wait_ge(z_ok, 2 * NT)
            pe.wait_ge(adj_lo_ok, NC)
            for j in range(CJ):
                ins = agg_part(c % 2, j, z_of(c * CJ + j), False)
            ins.then_inc(agg_chunk, 1)
            agg_end(0)

            def agg_quarter(q):
                pe.wait_ge(agg_free, q * QT)
                for u in range(2):
                    pe.wait_ge(adj_lo_ok, q * NC + u + 1)
                    for j in range(CJ):
                        ins = agg_part(u, j, z_of(u * CJ + j), u == 0 and j == 0)
                    ins.then_inc(agg_chunk, 1)
                with pe.Fori(1, NC // 2) as c:
                    for u in range(2):
                        pe.wait_ge(adj_lo_ok, c * 2 + (q * NC + u + 1))
                        for j in range(CJ):
                            ins = agg_part(u, j, z_of(c * (2 * CJ) + (u * CJ + j)), False)
                        ins.then_inc(agg_chunk, 1)
                agg_end(q)

            def xf_transposes(q):
                for it in range(QT):
                    t = q * QT + it
                    pe.wait_ge(ln_ready, NT + t + 1)
                    if it >= 2:
                        pe.wait_ge(xfT_lo_ok, t - 1)
                    elif it == 0:
                        pe.wait_ge(dinv_ok, q + 2 if q + 1 < NQ else NQ)
                        if q > 0:
                            pe.wait_ge(sh_gelu, shared_blocks_before[q])
                    transposes(bank[4 + t % 2], norm[:, t, :]).then_inc(xfT_ps, 1)

            def gate(q):
                if q > 0:
                    pe.wait_ge(sh_free, shared_halves_before[q] * 2)
                for it in range(QT):
                    t = q * QT + it
                    pe.wait_ge(xfT_lo_ok, t + 1)
                    if it >= 2:
                        pe.wait_ge(logit_ok, t - 1)
                    n = 0
                    for k in range(KD):
                        for a in (xfT_hi, xfT_lo):
                            ins = pe.matmul(bank[6 + t % 2][:, 0:HALF], a[:, q % 2, k, it * P:(it + 1) * P],
                                            gate_r[:, k, :], start=n == 0, stop=n == 2 * KD - 1)
                            n += 1
                    ins.then_inc(logit_ps, 1)

            def shared_up(m):
                hq, ib = m // NI, m % NI
                q, half = hq // 2, hq % 2
                if m >= 2:
                    pe.wait_ge(sh_gelu, m - 1)
                n = 0
                for k in range(KD):
                    for w, a in ((sw1_hi, xfT_hi), (sw1_hi, xfT_lo), (sw1_lo, xfT_hi)):
                        ins = pe.matmul(bank[4 + m % 2][:, 0:HALF], w[:, k, ib * P:(ib + 1) * P],
                                        a[:, q % 2, k, half * HALF:(half + 1) * HALF],
                                        start=n == 0, stop=n == 3 * KD - 1)
                        n += 1
                ins.then_inc(sh_ps, 1)

            def shared_down(m):
                hq, ib = m // NI, m % NI
                if ib == 0 and hq:
                    pe.wait_ge(sh_free, hq * 2)
                pe.wait_ge(sh_lo, m + 1)
                for k in range(2):
                    pe.matmul(bank[6 + k][:, :], gel_hi[:, m % 2, k * P:(k + 1) * P],
                              sw2_r[:, ib, :, :].rearrange("p h d -> p (h d)"), start=ib == 0, stop=False)
                    ins = pe.matmul(bank[6 + k][:, 0:D], gel_lo[:, m % 2, k * P:(k + 1) * P],
                                    sw2_r[:, ib, 0, :], start=False, stop=ib == NI - 1)
                ins.then_inc(sh_used, 1)

            def shared(first, n):
                for m in range(first, first + n + 2):
                    if m < first + n:
                        shared_up(m)
                    if m >= first + 2:
                        shared_down(m - 2)

            shared_blocks_before = {q: 2 * q * NI if q < NQ - 1 else (2 * NQ - 3) * NI for q in range(NQ)}
            shared_halves_before = {q: 2 * q if q < NQ - 1 else 2 * NQ - 3 for q in range(NQ)}
            for q in range(1, NQ):
                if q >= 2:
                    pe.wait_ge(sh_gelu, shared_blocks_before[q - 1])
                agg_quarter(q)
                xf_transposes(q - 1)
                pe.wait_ge(split_lo, 4)
                gate(q - 1)
                pe.wait_ge(logit_ok, q * QT)
                shared((q - 1) * 2 * NI, 2 * NI if q < NQ - 1 else NI)
            xf_transposes(NQ - 1)
            gate(NQ - 1)
            pe.wait_ge(logit_ok, NT)
            shared((2 * NQ - 3) * NI, NI)
            pe.wait_ge(hot_ok, 1)
            pe.wait_ge(sh_free, 2 * (2 * NQ - 2))
            flat = hot_b[:].rearrange("p t e -> p (t e)")
            pe.matmul(bank[6][:, 0:NT * E], ones[:], flat, start=True, stop=True)
            pe.matmul(bank[7][:, 0:NT * E], before[:], flat, start=True, stop=True).then_inc(rank_ps, 1)
            pe.wait_ge(rank_read, 1)
            shared((2 * NQ - 2) * NI, 2 * NI)

            def rows_transpose(u, loads):
                pe.wait_ge(xs_loaded[u], loads * 16)
                transposes(bank[7], xs[:, u, :]).then_inc(xsT_ps, 1)

            def up(s):
                chunks = pe.value_load(step_chunks[0:1, bass.ds(s, 1)], min_val=1, max_val=(E - 1) * EC)
                slot = pe.value_load(step_slot[0:1, bass.ds(s, 1)], min_val=0, max_val=1)
                pe.wait_ge(elo_ok, chunks)
                pe.wait_ge(xsT_lo_ok, s + 1)
                for h in range(IH):
                    if not isinstance(s, int) or s > 0:
                        pe.wait_ge(hid_ok, s * IH + (h - 1))
                    for w in range(2):
                        n = 0
                        for k in range(KD):
                            at = (w * KD + k) * I + h * BANK
                            for a, part in ((xsT_hi, 0), (xsT_lo, 0), (xsT_hi, 1)):
                                ins = pe.matmul(bank[2 * w + h][:, :], a[:, k, :],
                                                ering[:, bass.ds(slot, 1), part, at:at + BANK].rearrange(
                                                    "p a n -> p (a n)"),
                                                start=n == 0, stop=n == 3 * KD - 1)
                                n += 1
                    ins.then_inc(up_ps, 1)
                return slot

            def hid_transposes(s):
                for h in range(IH):
                    pe.wait_ge(hid_ok, s * IH + (h + 1))
                    for k in range(NI // IH):
                        ins = pe.transpose(bank[4 + h][:, k * P:(k + 1) * P],
                                           hid[:, h * BANK + k * P:h * BANK + (k + 1) * P], ident[:])
                    ins.then_inc(hidT_ps, 1)

            def down(s):
                slot = pe.value_load(step_slot[0:1, bass.ds(s, 1)], min_val=0, max_val=1)
                if not isinstance(s, int) or s > 0:
                    pe.wait_ge(y_ok, s)
                for k in range(NI):
                    if k % (NI // IH) == 0:
                        pe.wait_ge(hidT_lo_ok, s * IH + (k // (NI // IH) + 1))
                    w2 = ering[:, bass.ds(slot, 1), :, W2AT + k * D:W2AT + (k + 1) * D].rearrange("p a h n -> p (a h) n")
                    pe.matmul(bank[6][:, :], hidT_hi[:, k, :], w2, start=k == 0, stop=False)
                    ins = pe.matmul(bank[6][:, 0:D], hidT_lo[:, k, :],
                                    ering[:, bass.ds(slot, 1), 0, W2AT + k * D:W2AT + (k + 1) * D].rearrange(
                                        "p a n -> p (a n)"),
                                    start=False, stop=k == NI - 1)
                ins.then_inc(steps_done, 1)

            pe.wait_ge(sh_free, 2 * 2 * NQ)
            pe.wait_ge(elo0_ok, EC)
            pe.transpose(bank[7][:, 0:P], ident[:], ident[:]).then_inc(steps_done, 1)
            rows_transpose(0, 1)
            up(0)
            rows_transpose(1, 1)
            hid_transposes(0)
            def one_step(s, u, loads):
                up(s)
                if loads is not None:
                    rows_transpose(u, loads)
                down(s - 1)
                hid_transposes(s)

            for u in range(2):
                one_step(1 + u, u, 2)
            with pe.Fori(1, (STEPS - 3) // 2) as i:
                for u in range(2):
                    one_step(i * 2 + (1 + u), u, i + 2)
            for u in range(2):
                one_step(STEPS - 2 + u, u, (STEPS - 1) // 2 + 1 if u == 0 else None)
            down(STEPS - 1)


def kernel(x, adj, L0_gnn_W, L0_gnn_b, L0_ffn_gate_w, L0_ffn_w1, L0_ffn_w2, L0_ffn_w3, L0_ffn_sw1, L0_ffn_sw2):
    import numpy as np
    import concourse.bacc as bacc
    from concourse.bass_utils import run_bass_kernel_spmd

    def by_rows(w):
        e, r, n = w.shape
        return w.reshape(e, r // P, P, n).transpose(0, 2, 1, 3).reshape(e, P, -1)

    w1 = by_rows(np.asarray(L0_ffn_w1).transpose(0, 2, 1))
    w3 = by_rows(np.asarray(L0_ffn_w3).transpose(0, 2, 1))
    w2 = by_rows(np.asarray(L0_ffn_w2).transpose(0, 2, 1))
    arrays = {
        "x": np.asarray(x),
        "adj_t": np.asarray(adj).T,
        "gnn_w": np.asarray(L0_gnn_W),
        "gnn_b": np.asarray(L0_gnn_b),
        "gate_t": np.asarray(L0_ffn_gate_w).T,
        "experts": np.concatenate([w1, w3, w2], axis=2),
        "sw1_t": np.asarray(L0_ffn_sw1).T,
        "sw2_t": np.asarray(L0_ffn_sw2).T,
    }
    arrays = {f"in_{k}": np.ascontiguousarray(v) for k, v in arrays.items()}
    nc = bacc.Bacc("TRN2", target_bir_lowering=False, num_devices=1)
    args = [nc.dram_tensor(k, v.shape, mybir.dt.from_np(v.dtype), kind="ExternalInput").ap()
            for k, v in arrays.items()]
    out = nc.dram_tensor("out", np.asarray(x).shape, F32, kind="ExternalOutput").ap()
    gnn_moe(nc, *args, out)
    r = run_bass_kernel_spmd(nc, [arrays], core_ids=[0])
    return r.results[0]["out"]
```

```python
from contextlib import ExitStack

import concourse.bass as bass
from concourse import mybir

F32 = mybir.dt.float32
F32R = mybir.dt.float32r
BF16 = mybir.dt.bfloat16
I32 = mybir.dt.int32
U32 = mybir.dt.uint32
ALU = mybir.AluOpType
ACT = mybir.ActivationFunctionType
AX_X = mybir.AxisListType.X

P = 128
BANK = 512
EPS = 1e-5


def gnn_moe(nc, x_in, adj_t, w_in, b_in, gate_t, experts, sw1_t, sw2_t, out):
    N, D = x_in.shape
    E = gate_t.shape[1]
    I = sw1_t.shape[1]
    NT = N // P
    KD = D // P
    NI = I // P
    QT = BANK // P
    NQ = NT // QT
    CJ = 2
    NC = NT // CJ
    RAW = 4
    TURN = NT - 4
    AR = 4
    HALF = 2 * P
    NB = 2 * NQ * NI
    STEPS = NT + E - 1
    WCOL = experts.shape[2]
    W2AT = 2 * KD * I
    EC = 12
    ECW = WCOL // EC
    ER = 4
    EP = [0, W2AT // 4, W2AT, WCOL]
    EUP = W2AT // ECW
    IH = I // BANK
    assert KD == 2 and IH == 2 and NT == NQ * QT and RAW % 2 == 0 and NC % RAW == 0

    ROW = D + 2
    sorted_x = nc.dram_tensor("sorted_x", (STEPS * P, ROW), F32, kind="Internal").ap()

    base = (nc.sbuf_base + 31) // 32 * 32
    top = [base]
    size = {F32: 4, F32R: 4, BF16: 2, I32: 4, U32: 4}

    def place(name, shape, dtype, at=None):
        n = size[dtype]
        for k in shape[1:]:
            n *= k
        n = (n + 31) // 32 * 32
        where = top if at is None else at
        t = nc.alloc_sbuf_tensor_at(name, shape, dtype, offset=where[0])
        where[0] += n
        assert where[0] <= nc.sbuf_usable_end, (name, where[0])
        return t

    resid = place("resid", [P, NT, D], F32)
    y_at = [top[0]]
    rows = place("rows", [P, NT, ROW], F32)
    norm = rows[:, :, 0:D]
    xfT_hi = place("xfT_hi", [P, 2, KD, BANK], F32R)
    xfT_lo = place("xfT_lo", [P, 2, KD, BANK], F32R)
    y_rows = place("y_rows", [P, STEPS, D], F32, y_at)
    assert y_at[0] <= top[0]
    gel = place("gel", [P, 2, HALF], F32)
    gel_hi = place("gel_hi", [P, 2, HALF], F32R)
    gel_lo = place("gel_lo", [P, 2, HALF], F32R)
    xs = place("xs", [P, 2, D], F32)
    xsT_hi = place("xsT_hi", [P, KD, P], F32R)
    xsT_lo = place("xsT_lo", [P, KD, P], F32R)
    ident = place("ident", [P, P], F32)
    ident_r = place("ident_r", [P, P], F32R)
    ones = place("ones", [P, P], BF16)
    before = place("before", [P, P], BF16)
    gate_r = place("gate_r", [P, KD, HALF], F32R)
    gate_raw = place("gate_raw", [P, KD, E], F32)
    e_less = place("e_less", [P, NT, E], F32)
    k128 = place("k128", [P, E, NT], F32)
    s_iota = place("s_iota", [P, STEPS, E], F32)
    upto = place("upto", [P, E, E], F32)
    eps = place("eps", [P, 1], F32)
    stats = place("stats", [P, QT, 6], F32)
    mv = place("mv", [P, QT, 2], F32)
    rstd = place("rstd", [P, QT], F32)
    std = place("std", [P, QT], F32)
    deg = place("deg", [P, QT], F32)
    dinv2 = place("dinv2", [P, QT], F32)
    logit = place("logit", [P, NT, E], F32)
    top1 = place("top1", [P, NT], F32)
    choice = place("choice", [P, NT], F32)
    hot = place("hot", [P, NT, E], F32)
    hot_b = place("hot_b", [P, NT, E], BF16)
    rank = place("rank", [P, NT, E], F32)
    r_a = place("r_a", [P, NT, E], F32)
    scan = place("scan", [P, 2, NT // 2 + NT, E], F32)
    tiles = place("tiles", [P, E], F32)
    ends = place("ends", [P, E], F32)
    ebase = place("ebase", [P, E], F32)
    r_e = place("r_e", [P, E, NT], F32)
    r_s = place("r_s", [P, STEPS, E], F32)
    pos_f = place("pos_f", [P, NT], F32)
    pos = place("pos", [P, NT], U32)
    step_f = place("step_f", [P, STEPS], F32)
    step_chunks = place("step_chunks", [P, STEPS], I32)
    step_i = place("step_i", [P, STEPS], I32)
    step_slot = place("step_slot", [P, STEPS], I32)
    end_i = place("end_i", [P, E], I32)
    table_use = place("table_use", [P, 1], F32)
    wt_e = place("wt_e", [P, STEPS], F32)
    wt_r = place("wt_r", [P, STEPS], F32)
    meta = place("meta", [P, STEPS, 2], F32)
    row_wt = place("row_wt", [P, STEPS], F32)
    row_token = place("row_token", [P, STEPS], U32)
    sw_at = [top[0]]
    sw1_hi = place("sw1_hi", [P, KD, I], F32R)
    sw1_lo = place("sw1_lo", [P, KD, I], F32R)
    sw2_r = place("sw2_r", [P, NI, 2, D], F32R)
    sil = place("sil", [P, I], F32, sw_at)
    hid = place("hid", [P, I], F32, sw_at)
    hidT_hi = place("hidT_hi", [P, NI, P], F32R, sw_at)
    hidT_lo = place("hidT_lo", [P, NI, P], F32R, sw_at)
    assert sw_at[0] <= top[0]
    zero_at = [top[0]]
    eraw = place("eraw", [P, ER, ECW], F32)
    zeros = place("zeros", [P, ROW], F32, zero_at)
    front = [top[0]]
    ering = place("ering", [P, 2, 2, WCOL], F32R)
    zz = place("zz", [P, NT, 2, D], F32R, front)
    araw = place("araw", [P, RAW, CJ, BANK], F32, front)
    a_hi = place("a_hi", [P, AR, BANK], F32R, front)
    a_lo = place("a_lo", [P, AR, BANK], F32R, front)
    sw1_raw = place("sw1_raw", [P, KD, I], F32, front)
    sw2_raw = place("sw2_raw", [P, NI, D], F32, front)
    w_raw = place("w_raw", [P, KD, D], F32, front)
    w_hi = place("w_hi", [P, KD, D], F32R, front)
    w_lo = place("w_lo", [P, KD, D], F32R, front)
    bias = place("bias", [P, D], F32, front)
    agg_at = [front[0]]
    xnT_hi = place("xnT_hi", [P, 2, KD, P], F32R, front)
    xnT_lo = place("xnT_lo", [P, 2, KD, P], F32R, front)
    agg = place("agg", [P, QT, D], F32, agg_at)
    count = place("count", [P, 2, CJ, BANK], BF16, front)
    assert front[0] <= top[0], (front[0], top[0])

    LAST = (NQ - 2) * 2 * NI
    STD_AT, XF_AT, GATE_AT, RANKS_AT = 6, 8, 11, 13
    DVE_AT = 20

    with ExitStack() as ctx:
        bank = [ctx.enter_context(nc.psum_tensor(f"bank{i}", [P, BANK], F32)) for i in range(8)]

        def xf_bank(q, b):
            return bank[(0 if q == NQ - 1 else 4) + b]

        def logit_bank(q, b):
            return bank[(0 if q == NQ - 1 else 6) + b]

        def shared_bank(hq, k):
            return bank[(6 if hq % 2 else 2) + k]

        def sem(name):
            return ctx.enter_context(nc.semaphore(name))

        x_loaded = [sem(f"x_loaded{g}") for g in range(NQ)]
        bias_loaded = sem("bias_loaded")
        w_loaded = sem("w_loaded")
        shared_loaded = sem("shared_loaded")
        gate_loaded = sem("gate_loaded")
        adj_loaded = [sem(f"adj_loaded{r}") for r in range(RAW)]
        pad_zeroed = sem("pad_zeroed")
        consts = sem("consts")
        pool_self = sem("pool_self")
        dve_consts = sem("dve_consts")
        split_hi = sem("split_hi")
        split_lo = sem("split_lo")
        dve_self = sem("dve_self")
        var_ready = sem("var_ready")
        std_ready = sem("std_ready")
        ln_ready = sem("ln_ready")
        xnT_ps = sem("xnT_ps")
        xnT_hi_ok = sem("xnT_hi_ok")
        xnT_lo_ok = sem("xnT_lo_ok")
        z_ps = sem("z_ps")
        z_hi_ok = sem("z_hi_ok")
        z_ok = sem("z_ok")
        z_copied = sem("z_copied")
        bias_added = sem("bias_added")
        adj_hi_ok = sem("adj_hi_ok")
        adj_lo_ok = sem("adj_lo_ok")
        adj_counted = sem("adj_counted")
        agg_tile = sem("agg_tile")
        agg_sum = sem("agg_sum")
        deg_ps = sem("deg_ps")
        dinv_ok = sem("dinv_ok")
        agg_copied = sem("agg_copied")
        agg_free = sem("agg_free")
        xfT_ps = sem("xfT_ps")
        xfT_hi_ok = sem("xfT_hi_ok")
        xfT_lo_ok = sem("xfT_lo_ok")
        logit_ps = sem("logit_ps")
        logit_ok = sem("logit_ok")
        sh_ps = sem("sh_ps")
        sh_gelu = sem("sh_gelu")
        sh_hi = sem("sh_hi")
        sh_lo = sem("sh_lo")
        sh_used = sem("sh_used")
        sh_free = sem("sh_free")
        hot_ok = sem("hot_ok")
        rank_ps = sem("rank_ps")
        routed = sem("routed")
        top1_ok = sem("top1_ok")
        exp_ok = sem("exp_ok")
        scattered = sem("scattered")
        ehi_first = [sem(f"ehi_first{h}") for h in range(3)]
        ehi_loaded = [sem(f"ehi_loaded{h}") for h in range(3)]
        eraw_loaded = [sem(f"eraw_loaded{s}") for s in range(ER)]
        elo_ok = sem("elo_ok")
        xs_loaded = [sem(f"xs_loaded{s}") for s in range(2)]
        xsT_ps = sem("xsT_ps")
        xsT_hi_ok = sem("xsT_hi_ok")
        xsT_lo_ok = sem("xsT_lo_ok")
        up_ps = sem("up_ps")
        silu_ok = sem("silu_ok")
        hid_ok = sem("hid_ok")
        hidT_ps = sem("hidT_ps")
        hidT_hi_ok = sem("hidT_hi_ok")
        hidT_lo_ok = sem("hidT_lo_ok")
        steps_done = sem("steps_done")
        y_copied = sem("y_copied")
        y_ok = sem("y_ok")
        meta_loaded = sem("meta_loaded")
        token_ok = sem("token_ok")
        x2_stored = sem("x2_stored")
        out_stored = sem("out_stored")

        def acc(it):
            return bank[it]

        def two_tiles(xfT, q, b):
            return xfT[:, q % 2, :, b * HALF:(b + 1) * HALF].rearrange("p k (t n) -> p t k n", t=2)

        block = ctx.enter_context(nc.Block())

        @block.sync
        def _(sp):
            def rows_of_x(g):
                sp.dma_start(resid[:, g * QT:(g + 1) * QT, :],
                             x_in[g * QT * P:(g + 1) * QT * P, :].rearrange("(t p) d -> p t d", p=P)
                             ).then_inc(x_loaded[g], 16)

            def chunk(q, c, n):
                if n is not None:
                    sp.wait_ge(adj_lo_ok, (n - RAW + 1) * CJ)
                    sp.wait_ge(adj_counted, (n - RAW + 1) * CJ)
                src = adj_t[c * CJ * P:(c + 1) * CJ * P, bass.ds(q * BANK, BANK)]
                sp.dma_start(araw[:, c % RAW, :, :], src.rearrange("(j p) i -> p j i", p=P)
                             ).then_inc(adj_loaded[c % RAW], 16)

            rows_of_x(0)
            for c in range(NC):
                if c + 1 < NQ:
                    rows_of_x(c + 1)
                chunk(0, c, c if c >= RAW else None)
            with sp.Fori(1, NQ) as q:
                for c in range(NC):
                    chunk(q, c, q * NC + c)
            sp.wait_ge(pad_zeroed, 16)
            for e in range(E):
                for c in range(EC):
                    n = e * EC + c
                    if n >= ER:
                        sp.wait_ge(elo_ok, n - ER + 1)
                    sp.dma_start(eraw[:, c % ER, :], experts[e, :, c * ECW:(c + 1) * ECW]
                                 ).then_inc(eraw_loaded[c % ER], 16)

        @block.gpsimd
        def _(pool):
            selfs = [0]

            def then_wait(ins):
                selfs[0] += 1
                ins.then_inc(pool_self, 1)
                pool.wait_ge(pool_self, selfs[0])

            then_wait(pool.memset(ident[:], 0.0))
            pool.affine_select(out=ident[:], in_=ident[:], compare_op=ALU.not_equal, fill=1.0, base=0,
                               pattern=[[-1, P]], channel_multiplier=1).then_inc(consts, 1)
            then_wait(pool.memset(zeros[:], 0.0))
            pool.memset(zeros[:, D:D + 1], float(2 * NT * P)).then_inc(consts, 1)
            pool.iota(rows[:, :, D:D + 1], pattern=[[P, NT], [0, 1]], base=0, channel_multiplier=1,
                      allow_small_or_imprecise_dtypes=True).then_inc(consts, 1)
            then_wait(pool.memset(ones[:], 1.0))
            pool.affine_select(out=before[:], in_=ones[:], compare_op=ALU.is_gt, fill=0.0, base=0,
                               pattern=[[1, P]], channel_multiplier=-1).then_inc(consts, 1)
            then_wait(pool.memset(upto[:], 1.0))
            pool.affine_select(out=upto[:], in_=upto[:], compare_op=ALU.is_ge, fill=0.0, base=0,
                               pattern=[[1, E], [-1, E]], channel_multiplier=0).then_inc(consts, 1)
            pool.iota(e_less[:], pattern=[[0, NT], [1, E]], base=-E, channel_multiplier=0,
                      allow_small_or_imprecise_dtypes=True).then_inc(consts, 1)
            pool.iota(k128[:], pattern=[[0, E], [P, NT]], base=0, channel_multiplier=0,
                      allow_small_or_imprecise_dtypes=True).then_inc(consts, 1)
            pool.iota(s_iota[:], pattern=[[1, STEPS], [0, E]], base=0, channel_multiplier=0,
                      allow_small_or_imprecise_dtypes=True).then_inc(consts, 1)

            def adj_lows(q, first, last):
                for j in range(first, last):
                    adj_low(j % (RAW * CJ), q * NT + j)

            def adj_low(u, n):
                pool.wait_ge(adj_hi_ok, n + 1)
                pool.tensor_tensor(a_lo[:, u % AR, :], araw[:, u // CJ, u % CJ, :],
                                   a_hi[:, u % AR, :].bitcast(F32), ALU.subtract).then_inc(adj_lo_ok, 1)

            def first_lows():
                pool.wait_ge(bias_loaded, 16)
                for t in range(NT):
                    adj_low(t % (RAW * CJ), t)
                    pool.wait_ge(z_copied, t + 1)
                    pool.tensor_tensor(norm[:, t, :], norm[:, t, :], bias[:], ALU.add).then_inc(bias_added, 1)

            def shared_lows(first, n):
                if n == 0:
                    return
                def one(u, m):
                    pool.wait_ge(sh_hi, m + 1)
                    pool.tensor_tensor(gel_lo[:, u, :], gel[:, u, :], gel_hi[:, u, :].bitcast(F32),
                                       ALU.subtract).then_inc(sh_lo, 1)

                if n == 2:
                    for u in range(2):
                        one(u, first + u)
                else:
                    with pool.Fori(0, n // 2) as m:
                        for u in range(2):
                            one(u, m * 2 + (first + u))

            def expert_high(e, slot, h, loaded=ehi_loaded):
                src = experts[bass.ds(e, 1), :, :].rearrange("a p n -> (a p) n")
                pool.dma_start(ering[:, slot, 0, EP[h]:EP[h + 1]], src[:, EP[h]:EP[h + 1]]
                               ).then_inc(loaded[h], 16)

            def expert(e, slot, last=None):
                if last is not None:
                    pool.wait_ge(xsT_ps, last)
                    expert_high(e, slot, 0)
                    expert_high(e, slot, 1)
                for c in range(EC):
                    if c * ECW == EP[2] // 2 and last is not None:
                        pool.wait_ge(steps_done, last)
                        expert_high(e, slot, 2)
                    if c * ECW in EP:
                        pool.wait_ge(ehi_loaded[EP.index(c * ECW)], e * 16)
                    pool.wait_ge(eraw_loaded[c % ER], (e * (EC // ER) + (c // ER + 1)) * 16)
                    pool.tensor_tensor(ering[:, slot, 1, c * ECW:(c + 1) * ECW], eraw[:, c % ER, :],
                                       ering[:, slot, 0, c * ECW:(c + 1) * ECW].bitcast(F32),
                                       ALU.subtract).then_inc(elo_ok, 1)

            first_lows()
            adj_lows(1, 0, AR)
            for q in range(1, NQ):
                adj_lows(q, AR, NT)
                if q < NQ - 1:
                    shared_lows((q - 1) * 2 * NI, NI)
                    for j in range(AR):
                        adj_lows(q + 1, j, j + 1)
                        shared_lows((q - 1) * 2 * NI + NI + j * NI // AR, NI // AR)
            shared_lows(LAST, 2)
            pool.wait_ge(agg_free, NT)
            for h in range(3):
                expert_high(0, 0, h, ehi_first)
                shared_lows(LAST + 2 + 2 * h, 2)
            shared_lows(LAST + 8, XF_AT - 6)
            pool.wait_ge(ln_ready, 2 * NT)
            for h in range(3):
                expert_high(1, 1, h)
                shared_lows(LAST + XF_AT + 2 + 2 * h, 2)
            shared_lows(LAST + XF_AT + 8, DVE_AT - XF_AT - 8)
            pool.wait_ge(pad_zeroed, 16)
            pool.wait_ge(routed, 2)
            pool.wait_ge(top1_ok, 1)
            for t in range(NT):
                pool.indirect_dma_start(out=sorted_x, out_offset=bass.IndirectOffsetOnAxis(ap=pos[:, t:t + 1], axis=0),
                                        in_=rows[:, t, :], in_offset=None).then_inc(scattered, 16)
            pool.wait_ge(elo_ok, EC)
            expert(1, 1)
            with pool.Fori(1, E // 2) as pair:
                for u in range(2):
                    last = pool.value_load(end_i[0:1, bass.ds(pair * 2 + (u - 2), 1)], min_val=1, max_val=STEPS + 1)
                    expert(pair * 2 + u, u, last)
            pool.wait_ge(x2_stored, 16)
            pool.wait_ge(token_ok, 1)
            for s in range(STEPS):
                pool.wait_ge(y_ok, s + 1)
                pool.indirect_dma_start(out=out, out_offset=bass.IndirectOffsetOnAxis(ap=row_token[:, s:s + 1], axis=0),
                                        in_=y_rows[:, s, :], in_offset=None, bounds_check=NT * P - 1,
                                        oob_is_err=False, compute_op=ALU.add).then_inc(out_stored, 16)
            pool.wait_ge(out_stored, 16 * STEPS)

        @block.scalar
        def _(act):
            act.dma_start(w_raw[:], w_in.rearrange("(k p) n -> p k n", p=P)).then_inc(w_loaded, 16)
            act.dma_start(bias[:], b_in.rearrange("(a d) -> a d", a=1).partition_broadcast(P)
                          ).then_inc(bias_loaded, 16)
            def load_table(function):
                act.activation(table_use[:], eps[:], function)

            def stds(k):
                act.wait_ge(var_ready, QT * (k + 1))
                act.activation(std[:], mv[:, :, 1], ACT.Sqrt, bias=eps[:, 0:1]).then_inc(std_ready, 1)

            def xn_high(t):
                act.wait_ge(xnT_ps, t + 1)
                if t >= 2:
                    act.wait_ge(z_ps, t - 1)
                act.activation(xnT_hi[:, t % 2], bank[4 + t % 2][:, 0:D].rearrange("p (k n) -> p k n", k=KD),
                               ACT.Copy).then_inc(xnT_hi_ok, 1)

            def z_high(t):
                act.wait_ge(z_ps, t + 1)
                act.activation(zz[:, t, 0, :], bank[6 + t % 2][:, 0:D], ACT.Copy).then_inc(z_hi_ok, 1)
                act.activation(norm[:, t, :], bank[6 + t % 2][:, 0:D], ACT.Copy).then_inc(z_copied, 1)

            def adj_high(u, loads, used):
                act.wait_ge(adj_loaded[u // CJ], loads * 16)
                if used is not None:
                    act.wait_ge(agg_tile, used)
                act.activation(a_hi[:, u % AR, :], araw[:, u // CJ, u % CJ, :], ACT.Copy).then_inc(adj_hi_ok, 1)

            act.wait_ge(dve_consts, 1)
            load_table(ACT.Sqrt)
            stds(0)
            act.wait_ge(consts, 1)
            act.activation(ident_r[:], ident[:], ACT.Copy).then_inc(split_hi, 1)
            act.wait_ge(w_loaded, 16)
            act.activation(w_hi[:], w_raw[:], ACT.Copy).then_inc(split_hi, 1)
            xn_high(0)

            LATER = (6, 9)
            for t in range(NT):
                if t % QT == 2 and t // QT + 1 < NQ:
                    stds(t // QT + 1)
                if t + 1 < NT:
                    xn_high(t + 1)
                adj_high(t % (RAW * CJ), t // (RAW * CJ) + 1, t - AR + 1 if t >= AR else None)
                z_high(t)
                if t == LATER[0]:
                    act.dma_start(gate_raw[:], gate_t.rearrange("(k p) n -> p k n", p=P)).then_inc(gate_loaded, 16)
                    act.dma_start(sw1_raw[:], sw1_t.rearrange("(k p) n -> p k n", p=P)).then_inc(shared_loaded, 16)
                elif t == LATER[1]:
                    act.dma_start(sw2_raw[:], sw2_t.rearrange("(k p) n -> p k n", p=P)).then_inc(shared_loaded, 16)

            def adj_highs(q, first, last):
                for j in range(first, last):
                    n = q * NT + j
                    adj_high(n % (RAW * CJ), n // (RAW * CJ) + 1, n - AR + 1)

            def copy_sums(q):
                act.wait_ge(agg_sum, q + 1)
                for it in range(QT):
                    act.activation(agg[:, it, :], acc(it)[:, 0:D], ACT.Copy).then_inc(agg_copied, 1)

            def xfT_highs(q):
                for b in range(2):
                    act.wait_ge(xfT_ps, 2 * q + b + 1)
                    act.activation(two_tiles(xfT_hi, q, b),
                                   xf_bank(q, b)[:, :].rearrange("p (t k n) -> p t k n", t=2, k=KD),
                                   ACT.Copy).then_inc(xfT_hi_ok, 1)

            def shared_blocks(first, n):
                def one(u, m, early):
                    act.wait_ge(sh_ps, m + 1)
                    if not early:
                        act.wait_ge(sh_lo, m - 1)
                    act.activation(gel[:, u, :], bank[4 + u][:, 0:HALF], ACT.Gelu).then_inc(sh_gelu, 1)
                    act.wait_ge(sh_gelu, m + 1)
                    if not early:
                        act.wait_ge(sh_used, m - 1)
                    act.activation(gel_hi[:, u, :], gel[:, u, :], ACT.Copy).then_inc(sh_hi, 1)

                skip = 2 if first == 0 else 0
                for m in range(skip):
                    one(m, m, True)
                if n - skip == 2:
                    for u in range(2):
                        one(u, first + skip + u, False)
                else:
                    with act.Fori(0, (n - skip) // 2) as m:
                        for u in range(2):
                            one(u, m * 2 + (first + skip + u), False)

            def split_shared():
                act.wait_ge(gate_loaded, 16)
                act.wait_ge(dve_consts, 2)
                act.activation(gate_r[:, :, 0:E], gate_raw[:], ACT.Copy).then_inc(split_hi, 1)
                act.wait_ge(shared_loaded, 32)
                act.activation(sw1_hi[:], sw1_raw[:], ACT.Copy).then_inc(split_hi, 1)
                act.activation(sw2_r[:, :, 0, :], sw2_raw[:], ACT.Copy).then_inc(split_hi, 1)

            adj_highs(1, 0, AR)
            copy_sums(0)
            for q in range(1, NQ):
                if q == 1:
                    split_shared()
                adj_highs(q, AR, TURN)
                stds(NQ + q - 1)
                adj_highs(q, TURN, TURN + AR - 1)
                xfT_highs(q - 1)
                adj_highs(q, TURN + AR - 1, NT)
                copy_sums(q)
                load_table(ACT.Gelu)
                if q == 1:
                    act.wait_ge(consts, 2)
                    act.dma_start(sorted_x.rearrange("(s p) d -> p s d", p=P),
                                  zeros[:, :].rearrange("p (a d) -> p a d", a=1).to_broadcast([P, STEPS, ROW])
                                  ).then_inc(pad_zeroed, 16)
                if q < NQ - 1:
                    shared_blocks((q - 1) * 2 * NI, NI)
                    for j in range(AR):
                        adj_highs(q + 1, j, j + 1)
                        shared_blocks((q - 1) * 2 * NI + NI + j * NI // AR, NI // AR)
            shared_blocks(LAST, STD_AT)
            stds(2 * NQ - 1)
            shared_blocks(LAST + STD_AT, XF_AT - STD_AT)
            xfT_highs(NQ - 1)
            shared_blocks(LAST + XF_AT, 4 * NI - XF_AT)

            def load_rows(s, u, dep):
                if dep is not None:
                    act.wait_ge(xsT_ps, dep)
                act.dma_start(xs[:, u, :], sorted_x[bass.ds(s * P, P), 0:D]).then_inc(xs_loaded[u], 16)

            def rows_high(n):
                act.wait_ge(xsT_ps, n)
                act.activation(xsT_hi[:], bank[7][:, 0:D].rearrange("p (k n) -> p k n", k=KD), ACT.Copy
                               ).then_inc(xsT_hi_ok, 1)

            def silus(s):
                for h in range(IH):
                    act.wait_ge(up_ps, s * IH + (h + 1))
                    act.activation(sil[:, h * BANK:(h + 1) * BANK], bank[h][:, :], ACT.Silu).then_inc(silu_ok, 1)

            def y_copy(s):
                act.wait_ge(steps_done, s + 2)
                act.activation(y_rows[:, bass.ds(s, 1), :].rearrange("p a d -> p (a d)"), bank[6][:, 0:D],
                               ACT.Copy).then_inc(y_copied, 1)

            def hid_highs(s):
                for h in range(IH):
                    act.wait_ge(hidT_ps, s * IH + (h + 1))
                    act.activation(hidT_hi[:, h * 4:(h + 1) * 4, :],
                                   bank[4 + h][:, :].rearrange("p (k n) -> p k n", n=P), ACT.Copy
                                   ).then_inc(hidT_hi_ok, 1)

            def step(s, u):
                if not isinstance(s, int) or s + 2 < STEPS:
                    load_rows(s + 2, 1 - u, s + 1)
                silus(s)
                if not isinstance(s, int) or s + 1 < STEPS:
                    rows_high(s + 2)
                y_copy(s - 1)
                hid_highs(s)

            act.wait_ge(scattered, 16 * NT)
            load_rows(0, 0, None)
            load_rows(1, 1, None)
            act.dma_start(meta[:], sorted_x.rearrange("(s p) d -> p s d", p=P)[:, :, D:ROW]
                          ).then_inc(meta_loaded, 16)
            rows_high(1)
            load_rows(2, 0, 1)
            act.wait_ge(meta_loaded, 16)
            act.activation(wt_e[:], meta[:, :, 1], ACT.Exp).then_inc(exp_ok, 1)
            silus(0)
            rows_high(2)
            act.wait_ge(sh_free, 2 * 2 * NQ)
            act.dma_start(out.rearrange("(t p) d -> p t d", p=P), resid[:]).then_inc(x2_stored, 16)
            hid_highs(0)
            with act.Fori(0, (STEPS - 3) // 2) as i:
                for u in range(2):
                    step(i * 2 + (1 + u), u)
            for u in range(2):
                step(STEPS - 2 + u, u)
            y_copy(STEPS - 1)

        @block.vector
        def _(dve):
            selfs = [0]

            def chained(ins):
                selfs[0] += 1
                ins.then_inc(dve_self, 1)

            def settle():
                dve.wait_ge(dve_self, selfs[0])

            dve.memset(eps[:], EPS).then_inc(dve_consts, 1)
            dve.memset(gate_r[:].bitcast(F32), 0.0).then_inc(dve_consts, 1)
            chained(dve.memset(scan[:], 0.0))

            def statistics(tiles_of, first, last):
                for i in range(first, last):
                    chained(dve.bn_stats(stats[:, i, :], resid[:, tiles_of[i], :]))

            def aggregates():
                settle()
                for i in range(QT):
                    dve.bn_aggr(mv[:, i, :], stats[:, i, :]).then_inc(var_ready, 1)

            def variances(tiles_of):
                statistics(tiles_of, 0, QT)
                aggregates()

            def normalize(k, tiles_of, first=0, last=QT):
                if first == 0:
                    dve.wait_ge(std_ready, k + 1)
                    chained(dve.reciprocal(rstd[:], std[:]))
                    settle()
                for i, t in list(enumerate(tiles_of))[first:last]:
                    dve.tensor_scalar(norm[:, t, :], resid[:, t, :], mv[:, i, 0:1], rstd[:, i:i + 1],
                                      ALU.subtract, ALU.mult).then_inc(ln_ready, 1)

            def group(q):
                return range(q * QT, (q + 1) * QT)

            def xn_low(t):
                dve.wait_ge(xnT_hi_ok, t + 1)
                dve.tensor_tensor(xnT_lo[:, t % 2], bank[4 + t % 2][:, 0:D].rearrange("p (k n) -> p k n", k=KD),
                                  xnT_hi[:, t % 2].bitcast(F32), ALU.subtract).then_inc(xnT_lo_ok, 1)

            def z_low(t):
                dve.wait_ge(z_hi_ok, t + 1)
                dve.wait_ge(z_copied, t + 1)
                dve.tensor_tensor(zz[:, t, 1, :], bank[6 + t % 2][:, 0:D], zz[:, t, 0, :].bitcast(F32),
                                  ALU.subtract).then_inc(z_ok, 1)

            def count_chunk(q, r, loads, n, first):
                dve.wait_ge(adj_loaded[r], loads * 16)
                into = count[:, q % 2, :, :]
                if first:
                    dve.tensor_scalar(into, araw[:, r, :, :], 0.0, None, ALU.not_equal).then_inc(adj_counted, CJ)
                else:
                    dve.wait_ge(adj_counted, n * CJ)
                    dve.scalar_tensor_tensor(into, araw[:, r, :, :], 0.0, into, ALU.not_equal, ALU.add
                                             ).then_inc(adj_counted, CJ)

            dve.wait_ge(x_loaded[0], 16)
            variances(group(0))
            normalize(0, group(0))
            dve.wait_ge(w_loaded, 16)
            dve.wait_ge(split_hi, 2)
            dve.tensor_tensor(w_lo[:], w_raw[:], w_hi[:].bitcast(F32), ALU.subtract).then_inc(split_lo, 1)
            xn_low(0)
            for t in range(NT):
                if t + 1 < NT:
                    xn_low(t + 1)
                g, i = t // QT + 1, t % QT
                if g < NQ and i == 0:
                    dve.wait_ge(x_loaded[g], 16)
                    dve.wait_ge(ln_ready, g * QT)
                if g < NQ and i < 2:
                    statistics(group(g), 2 * i, 2 * i + 2)
                elif g < NQ:
                    normalize(g, group(g), 2 * (i - 2), 2 * (i - 1))
                z_low(t)
                if g < NQ and i == 1:
                    aggregates()
                if t % CJ == CJ - 1:
                    c = t // CJ
                    count_chunk(0, c % RAW, c // RAW + 1, c, c == 0)

            def split_shared():
                dve.wait_ge(split_hi, 3)
                dve.tensor_tensor(gate_r[:, :, E:2 * E], gate_raw[:], gate_r[:, :, 0:E].bitcast(F32),
                                  ALU.subtract).then_inc(split_lo, 1)
                dve.wait_ge(split_hi, 5)
                dve.tensor_tensor(sw1_lo[:], sw1_raw[:], sw1_hi[:].bitcast(F32), ALU.subtract
                                  ).then_inc(split_lo, 1)
                dve.tensor_tensor(sw2_r[:, :, 1, :], sw2_raw[:], sw2_r[:, :, 0, :].bitcast(F32),
                                  ALU.subtract).then_inc(split_lo, 1)

            def count_chunks(q, first, last):
                for c in range(first, last):
                    n = q * NC + c
                    count_chunk(q, c % RAW, n // RAW + 1, n, c == 0)

            def inverse_degree(q):
                dve.wait_ge(deg_ps, q + 1)
                chained(dve.tensor_scalar(deg[:], bank[5][:, 0:QT], 1.0, None, ALU.max))
                settle()
                dve.reciprocal(dinv2[:], deg[:]).then_inc(dinv_ok, 1)

            def finish_gnn(q):
                for it in range(QT):
                    dve.wait_ge(agg_copied, q * QT + it + 1)
                    dve.tensor_tensor(agg[:, it, :], acc(it)[:, D:2 * D], agg[:, it, :], ALU.add
                                      ).then_inc(agg_free, 1)
                dve.wait_ge(agg_free, (q + 1) * QT)
                dve.wait_ge(dinv_ok, q + 1)
                dve.wait_ge(bias_added, (q + 1) * QT)
                for it, t in enumerate(group(q)):
                    chained(dve.scalar_tensor_tensor(agg[:, it, :], agg[:, it, :], dinv2[:, it:it + 1],
                                                     norm[:, t, :], ALU.mult, ALU.add))
                settle()
                for it, t in enumerate(group(q)):
                    chained(dve.scalar_tensor_tensor(resid[:, t, :], agg[:, it, :], 0.0, resid[:, t, :],
                                                     ALU.max, ALU.add))
                settle()

            def xfT_lows(q):
                for b in range(2):
                    dve.wait_ge(xfT_hi_ok, 2 * q + b + 1)
                    dve.tensor_tensor(two_tiles(xfT_lo, q, b),
                                      xf_bank(q, b)[:, :].rearrange("p (t k n) -> p t k n", t=2, k=KD),
                                      two_tiles(xfT_hi, q, b).bitcast(F32),
                                      ALU.subtract).then_inc(xfT_lo_ok, 1)

            def logits(q):
                def part(b, w):
                    return logit_bank(q, b)[:, :].rearrange("p (t n) -> p t n", t=2)[:, :, w * E:(w + 1) * E]

                dve.wait_ge(logit_ps, q + 1)
                for b in range(2):
                    chained(dve.tensor_copy(logit[:, q * QT + 2 * b:q * QT + 2 * b + 2, :], part(b, 1)))
                settle()
                for b in range(2):
                    at = logit[:, q * QT + 2 * b:q * QT + 2 * b + 2, :]
                    dve.tensor_tensor(at, part(b, 0), at, ALU.add).then_inc(logit_ok, 1)

            def add_shared(hq):
                dve.wait_ge(sh_used, (hq + 1) * NI)
                for k in range(2):
                    chained(dve.tensor_tensor(resid[:, hq * 2 + k, :], shared_bank(hq, k)[:, 0:D],
                                              resid[:, hq * 2 + k, :], ALU.add))
                settle()
                for k in range(2):
                    dve.tensor_tensor(resid[:, hq * 2 + k, :], shared_bank(hq, k)[:, D:2 * D],
                                      resid[:, hq * 2 + k, :], ALU.add).then_inc(sh_free, 1)

            inverse_degree(0)
            finish_gnn(0)
            for q in range(1, NQ):
                count_chunks(q, 0, RAW)
                if q > 1:
                    dve.wait_ge(ln_ready, NT + (q - 1) * QT)
                variances(group(q - 1))
                if q == 1:
                    split_shared()
                normalize(NQ + q - 1, group(q - 1))
                xfT_lows(q - 1)
                count_chunks(q, RAW, NC)
                logits(q - 1)
                inverse_degree(q)
                finish_gnn(q)
                if q < NQ - 1:
                    add_shared(2 * (q - 1))
                    add_shared(2 * (q - 1) + 1)
            dve.wait_ge(ln_ready, NT + (NQ - 1) * QT)
            variances(group(NQ - 1))
            normalize(2 * NQ - 1, group(NQ - 1))
            xfT_lows(NQ - 1)
            logits(NQ - 1)

            dve.wait_ge(logit_ok, 2 * NQ)
            dve.wait_ge(consts, 8)

            def step(ins):
                chained(ins)
                settle()

            def over_e(ap):
                return ap.rearrange("p (t a) -> p t a", a=1).to_broadcast([P, NT, E])

            step(dve.tensor_reduce(top1[:], logit[:], AX_X, ALU.max))
            step(dve.tensor_tensor(hot[:], logit[:], over_e(top1[:]), ALU.is_equal))
            step(dve.tensor_tensor(r_a[:], hot[:], e_less[:], ALU.mult))
            step(dve.tensor_reduce(choice[:], r_a[:], AX_X, ALU.min))
            step(dve.tensor_tensor(hot[:], e_less[:], over_e(choice[:]), ALU.is_equal))
            dve.tensor_copy(hot_b[:], hot[:]).then_inc(hot_ok, 1)
            dve.tensor_tensor(rows[:, :, D + 1], top1[:], top1[:], ALU.subtract).then_inc(top1_ok, 1)
            add_shared(2 * (NQ - 2))
            dve.wait_ge(rank_ps, 1)
            ZT = NT // 2
            step(dve.tensor_copy(scan[:, 0, ZT:, :], bank[0][:, 0:NT * E].rearrange("p (t e) -> p t e", e=E)))
            step(dve.tensor_tensor(rank[:], bank[1][:, 0:NT * E].rearrange("p (t e) -> p t e", e=E),
                                   scan[:, 0, ZT:, :], ALU.subtract))
            a = 0
            for sh in (1, 2, 4, 8):
                step(dve.tensor_tensor(scan[:, 1 - a, ZT:, :], scan[:, a, ZT:, :],
                                       scan[:, a, ZT - sh:ZT - sh + NT, :], ALU.add))
                a = 1 - a
            total = scan[:, a, ZT + NT - 1, :]
            step(dve.tensor_tensor(r_e[:], total.rearrange("p (e a) -> p e a", a=1).to_broadcast([P, E, NT]),
                                   k128[:], ALU.is_gt))
            step(dve.tensor_reduce(tiles[:], r_e[:], AX_X, ALU.add))
            step(dve.tensor_scalar(tiles[:], tiles[:], 1.0, None, ALU.max))
            step(dve.tensor_tensor(r_e[:, :, 0:E],
                                   tiles[:].rearrange("p (a e) -> p a e", a=1).to_broadcast([P, E, E]),
                                   upto[:], ALU.mult))
            step(dve.tensor_reduce(ends[:], r_e[:, :, 0:E], AX_X, ALU.add))
            step(dve.tensor_tensor(ebase[:], ends[:], tiles[:], ALU.subtract))
            step(dve.tensor_tensor(r_a[:], scan[:, a, ZT:, :], rank[:], ALU.add))
            step(dve.tensor_scalar(ebase[:], ebase[:], float(P), None, ALU.mult))
            step(dve.tensor_tensor(r_a[:], r_a[:],
                                   ebase[:].rearrange("p (a e) -> p a e", a=1).to_broadcast([P, NT, E]), ALU.add))
            step(dve.tensor_tensor(r_a[:], r_a[:], hot[:], ALU.mult))
            step(dve.tensor_reduce(pos_f[:], r_a[:], AX_X, ALU.add))
            dve.tensor_copy(pos[:], pos_f[:]).then_inc(routed, 1)
            step(dve.tensor_tensor(r_s[:], ends[:].rearrange("p (a e) -> p a e", a=1).to_broadcast([P, STEPS, E]),
                                   s_iota[:], ALU.is_le))
            step(dve.tensor_reduce(step_f[:], r_s[:], AX_X, ALU.add))
            step(dve.tensor_scalar(step_i[:], step_f[:], float(E - 1), None, ALU.min))
            step(dve.tensor_scalar(step_slot[:], step_i[:], 1, None, ALU.bitwise_and))
            step(dve.tensor_scalar(step_f[:], step_f[:], float(E - 1), float(EC), ALU.min, ALU.mult))
            step(dve.tensor_scalar(step_chunks[:], step_f[:], float(EUP), None, ALU.add))
            dve.tensor_scalar(end_i[:], ends[:], 1.0, None, ALU.add).then_inc(routed, 1)
            add_shared(2 * NQ - 3)
            dve.wait_ge(sh_used, LAST + DVE_AT)
            for m in range(LAST + DVE_AT, NB):
                if m == NB - NI + 2:
                    add_shared(2 * NQ - 2)
                dve.wait_ge(sh_hi, m + 1)
                dve.tensor_tensor(gel_lo[:, m % 2, :], gel[:, m % 2, :], gel_hi[:, m % 2, :].bitcast(F32),
                                  ALU.subtract).then_inc(sh_lo, 1)
                c = m - (LAST + DVE_AT)
                if c < EC:
                    if c * ECW in EP:
                        dve.wait_ge(ehi_first[EP.index(c * ECW)], 16)
                    dve.wait_ge(eraw_loaded[c % ER], (c // ER + 1) * 16)
                    dve.tensor_tensor(ering[:, 0, 1, c * ECW:(c + 1) * ECW], eraw[:, c % ER, :],
                                      ering[:, 0, 0, c * ECW:(c + 1) * ECW].bitcast(F32),
                                      ALU.subtract).then_inc(elo_ok, 1)
            add_shared(2 * NQ - 1)

            def rows_low(n):
                dve.wait_ge(xsT_hi_ok, n)
                dve.tensor_tensor(xsT_lo[:], bank[7][:, 0:D].rearrange("p (k n) -> p k n", k=KD),
                                  xsT_hi[:].bitcast(F32), ALU.subtract).then_inc(xsT_lo_ok, 1)

            def hids(s):
                for h in range(IH):
                    dve.wait_ge(silu_ok, s * IH + (h + 1))
                    dve.scalar_tensor_tensor(hid[:, h * BANK:(h + 1) * BANK], bank[2 + h][:, :],
                                             row_wt[:, bass.ds(s, 1)],
                                             sil[:, h * BANK:(h + 1) * BANK], ALU.mult, ALU.mult
                                             ).then_inc(hid_ok, 1)

            def hid_lows(s):
                for h in range(IH):
                    dve.wait_ge(hidT_hi_ok, s * IH + (h + 1))
                    dve.tensor_tensor(hidT_lo[:, h * 4:(h + 1) * 4, :],
                                      bank[4 + h][:, :].rearrange("p (k n) -> p k n", n=P),
                                      hidT_hi[:, h * 4:(h + 1) * 4, :].bitcast(F32), ALU.subtract
                                      ).then_inc(hidT_lo_ok, 1)

            def y_add(s):
                dve.wait_ge(y_copied, s + 1)
                y = y_rows[:, bass.ds(s, 1), :].rearrange("p a d -> p (a d)")
                dve.tensor_tensor(y, bank[6][:, D:2 * D], y, ALU.add).then_inc(y_ok, 1)

            rows_low(1)
            dve.wait_ge(meta_loaded, 16)
            dve.tensor_copy(row_token[:], meta[:, :, 0]).then_inc(token_ok, 1)
            dve.wait_ge(exp_ok, 1)
            step(dve.reciprocal(wt_r[:], wt_e[:]))
            step(dve.tensor_tensor(row_wt[:], wt_e[:], wt_r[:], ALU.mult))
            hids(0)
            rows_low(2)
            hid_lows(0)
            def one_step(s, more):
                hids(s)
                if more:
                    rows_low(s + 2)
                y_add(s - 1)
                hid_lows(s)

            with dve.Fori(0, (STEPS - 3) // 2) as i:
                for u in range(2):
                    one_step(i * 2 + (1 + u), True)
            for u in range(2):
                one_step(STEPS - 2 + u, u == 0)
            y_add(STEPS - 1)

        @block.tensor
        def _(pe):
            def transposes(into, source):
                for k in range(KD):
                    ins = pe.transpose(into[:, k * P:(k + 1) * P], source[:, k * P:(k + 1) * P], ident[:])
                return ins

            def keep_clock_up(n):
                for _ in range(n):
                    pe.transpose(bank[0][:, 0:P], ident[:], ident[:])

            def xn_transpose(t):
                pe.wait_ge(ln_ready, t + 1)
                if t >= 2:
                    pe.wait_ge(xnT_lo_ok, t - 1)
                transposes(bank[4 + t % 2], norm[:, t, :]).then_inc(xnT_ps, 1)

            def z_tile(t):
                pe.wait_ge(xnT_lo_ok, t + 1)
                if t >= 2:
                    pe.wait_ge(z_ok, t - 1)
                    pe.wait_ge(z_copied, t - 1)
                n = 0
                for k in range(KD):
                    for a, w in ((xnT_hi, w_hi), (xnT_lo, w_hi), (xnT_hi, w_lo)):
                        ins = pe.matmul(bank[6 + t % 2][:, 0:D], a[:, t % 2, k, :], w[:, k, :],
                                        start=n == 0, stop=n == 3 * KD - 1)
                        n += 1
                ins.then_inc(z_ps, 1)

            def agg_part(j, s, n, first=False):
                pe.wait_ge(adj_lo_ok, n + 1)
                zt = zz[:, bass.ds(j, 1), :, :].rearrange("p a h d -> p (a h d)")
                for it in range(QT):
                    if first and not (isinstance(n, int) and n == 0):
                        pe.wait_ge(agg_free, n // NT * QT - QT + it + 1)
                    if first and it == 2 and n >= 2 * NT:
                        pe.wait_ge(sh_free, (2 * (n // NT - 2) + 1) * 2)
                    pe.matmul(acc(it)[:, :], a_hi[:, s, it * P:(it + 1) * P], zt,
                              start=first, stop=False)
                    ins = pe.matmul(acc(it)[:, 0:D], a_lo[:, s, it * P:(it + 1) * P], zt[:, 0:D],
                                    start=False, stop=False)
                ins.then_inc(agg_tile, 1)

            def agg_end(q):
                for it in range(QT):
                    ins = pe.matmul(acc(it)[:, :], ident_r[:], zz[:, q * QT + it, :, :].rearrange("p h d -> p (h d)"),
                                    start=False, stop=True)
                ins.then_inc(agg_sum, 1)

            def degrees(q):
                pe.wait_ge(adj_counted, (q + 1) * NT)
                for it in range(QT):
                    for j in range(CJ):
                        ins = pe.matmul(bank[5][:, it:it + 1], count[:, q % 2, j, it * P:(it + 1) * P],
                                        ones[:, 0:1], start=j == 0, stop=j == CJ - 1)
                ins.then_inc(deg_ps, 1)

            pe.wait_ge(consts, 4)
            keep_clock_up(20)
            xn_transpose(0)
            pe.wait_ge(split_lo, 1)
            for t in range(NT):
                if t + 1 < NT:
                    xn_transpose(t + 1)
                z_tile(t)
                if t >= 2:
                    pe.wait_ge(z_ok, t - 1)
                    agg_part(t - 2, (t - 2) % AR, t - 2, t == 2)
            for t in range(NT - 2, NT):
                pe.wait_ge(z_ok, t + 1)
                agg_part(t, t % AR, t)
            pe.wait_ge(z_copied, NT)
            agg_end(0)
            degrees(0)

            def agg_quarter(q):
                for u in range(AR):
                    agg_part(u, u, q * NT + u, u == 0)
                with pe.Fori(1, TURN // AR) as c:
                    for u in range(AR):
                        agg_part(c * AR + u, u, c * AR + (q * NT + u))
                xf_transposes(q - 1)
                for j in range(TURN, NT):
                    agg_part(j, j % AR, q * NT + j)
                agg_end(q)

            def xf_transposes(q):
                if q == NQ - 1:
                    pe.wait_ge(agg_free, NT)
                elif q > 0:
                    pe.wait_ge(sh_gelu, 2 * q * NI)
                for it in range(QT):
                    t = q * QT + it
                    pe.wait_ge(ln_ready, NT + t + 1)
                    ins = transposes(xf_bank(q, it // 2)[:, (it % 2) * D:(it % 2 + 1) * D], norm[:, t, :])
                    if it % 2:
                        ins.then_inc(xfT_ps, 1)

            def gate(q):
                if 0 < q < NQ - 1:
                    pe.wait_ge(sh_free, 2 * q * 2)
                for it in range(QT):
                    pe.wait_ge(xfT_lo_ok, 2 * q + (2 if q == NQ - 1 else it // 2 + 1))
                    n = 0
                    for k in range(KD):
                        for a in (xfT_hi, xfT_lo):
                            ins = pe.matmul(logit_bank(q, it // 2)[:, (it % 2) * HALF:(it % 2 + 1) * HALF],
                                            a[:, q % 2, k, it * P:(it + 1) * P],
                                            gate_r[:, k, :], start=n == 0, stop=n == 2 * KD - 1)
                            n += 1
                ins.then_inc(logit_ps, 1)

            def shared_up(m):
                hq, ib = m // NI, m % NI
                q, half = hq // 2, hq % 2
                if m >= 2:
                    pe.wait_ge(sh_gelu, m - 1)
                n = 0
                for k in range(KD):
                    for w, a in ((sw1_hi, xfT_hi), (sw1_hi, xfT_lo), (sw1_lo, xfT_hi)):
                        ins = pe.matmul(bank[4 + m % 2][:, 0:HALF], w[:, k, ib * P:(ib + 1) * P],
                                        a[:, q % 2, k, half * HALF:(half + 1) * HALF],
                                        start=n == 0, stop=n == 3 * KD - 1)
                        n += 1
                ins.then_inc(sh_ps, 1)

            def shared_down(m):
                hq, ib = m // NI, m % NI
                if ib == 0:
                    if hq % 2:
                        pe.wait_ge(logit_ok, 2 * min(hq // 2 + 1, NQ - 1))
                    else:
                        pe.wait_ge(agg_free, QT * min(hq // 2 + 2, NQ))
                    if hq >= 2:
                        pe.wait_ge(sh_free, (hq - 1) * 2)
                pe.wait_ge(sh_lo, m + 1)
                for k in range(2):
                    pe.matmul(shared_bank(hq, k)[:, :], gel_hi[:, m % 2, k * P:(k + 1) * P],
                              sw2_r[:, ib, :, :].rearrange("p h d -> p (h d)"), start=ib == 0, stop=False)
                    ins = pe.matmul(shared_bank(hq, k)[:, 0:D], gel_lo[:, m % 2, k * P:(k + 1) * P],
                                    sw2_r[:, ib, 0, :], start=False, stop=ib == NI - 1)
                ins.then_inc(sh_used, 1)

            def shared(first, n, between={}):
                for m in range(first, first + n + 2):
                    if m - first in between:
                        between[m - first]()
                    if m < first + n:
                        shared_up(m)
                    if m >= first + 2:
                        shared_down(m - 2)

            def ranks():
                pe.wait_ge(hot_ok, 1)
                flat = hot_b[:].rearrange("p t e -> p (t e)")
                pe.matmul(bank[0][:, 0:NT * E], ones[:], flat, start=True, stop=True)
                pe.matmul(bank[1][:, 0:NT * E], before[:], flat, start=True, stop=True).then_inc(rank_ps, 1)

            def degrees_read(q):
                return lambda: pe.wait_ge(dinv_ok, q + 1)

            for q in range(1, NQ):
                agg_quarter(q)
                pe.wait_ge(split_lo, 4)
                gate(q - 1)
                degrees(q)
                if q < NQ - 1:
                    shared((q - 1) * 2 * NI, 2 * NI, {1: degrees_read(q)})
            shared(LAST, 4 * NI, {1: degrees_read(NQ - 1), XF_AT: lambda: xf_transposes(NQ - 1), GATE_AT: lambda: gate(NQ - 1),
                                  RANKS_AT: ranks})

            def rows_transpose(u, loads):
                pe.wait_ge(xs_loaded[u], loads * 16)
                transposes(bank[7], xs[:, u, :]).then_inc(xsT_ps, 1)

            def up(s):
                chunks = pe.value_load(step_chunks[0:1, bass.ds(s, 1)], min_val=EUP, max_val=E * EC)
                slot = pe.value_load(step_slot[0:1, bass.ds(s, 1)], min_val=0, max_val=1)
                pe.wait_ge(elo_ok, chunks)
                pe.wait_ge(xsT_lo_ok, s + 1)
                for h in range(IH):
                    if not isinstance(s, int) or s > 0:
                        pe.wait_ge(hid_ok, s * IH + (h - 1))
                    for w in range(2):
                        n = 0
                        for k in range(KD):
                            at = (w * KD + k) * I + h * BANK
                            for a, part in ((xsT_hi, 0), (xsT_lo, 0), (xsT_hi, 1)):
                                ins = pe.matmul(bank[2 * w + h][:, :], a[:, k, :],
                                                ering[:, bass.ds(slot, 1), part, at:at + BANK].rearrange(
                                                    "p a n -> p (a n)"),
                                                start=n == 0, stop=n == 3 * KD - 1)
                                n += 1
                    ins.then_inc(up_ps, 1)

            def hid_transposes(s):
                for h in range(IH):
                    pe.wait_ge(hid_ok, s * IH + (h + 1))
                    for k in range(NI // IH):
                        ins = pe.transpose(bank[4 + h][:, k * P:(k + 1) * P],
                                           hid[:, h * BANK + k * P:h * BANK + (k + 1) * P], ident[:])
                    ins.then_inc(hidT_ps, 1)

            def down(s):
                chunks = pe.value_load(step_chunks[0:1, bass.ds(s, 1)], min_val=EUP, max_val=E * EC)
                slot = pe.value_load(step_slot[0:1, bass.ds(s, 1)], min_val=0, max_val=1)
                pe.wait_ge(elo_ok, chunks + (EC - EUP))
                if not isinstance(s, int) or s > 0:
                    pe.wait_ge(y_ok, s)
                for k in range(NI):
                    if k % (NI // IH) == 0:
                        pe.wait_ge(hidT_lo_ok, s * IH + (k // (NI // IH) + 1))
                    w2 = ering[:, bass.ds(slot, 1), :, W2AT + k * D:W2AT + (k + 1) * D].rearrange("p a h n -> p (a h) n")
                    pe.matmul(bank[6][:, :], hidT_hi[:, k, :], w2, start=k == 0, stop=False)
                    ins = pe.matmul(bank[6][:, 0:D], hidT_lo[:, k, :],
                                    ering[:, bass.ds(slot, 1), 0, W2AT + k * D:W2AT + (k + 1) * D].rearrange(
                                        "p a n -> p (a n)"),
                                    start=False, stop=k == NI - 1)
                ins.then_inc(steps_done, 1)

            pe.wait_ge(routed, 1)
            keep_clock_up(34)
            pe.wait_ge(sh_free, 2 * 2 * NQ)
            pe.transpose(bank[7][:, 0:P], ident[:], ident[:]).then_inc(steps_done, 1)
            rows_transpose(0, 1)
            up(0)
            rows_transpose(1, 1)
            hid_transposes(0)
            def one_step(s, u, loads):
                up(s)
                if loads is not None:
                    rows_transpose(u, loads)
                else:
                    pe.transpose(bank[7][:, 0:P], ident[:], ident[:]).then_inc(xsT_ps, 1)
                down(s - 1)
                hid_transposes(s)

            for u in range(2):
                one_step(1 + u, u, 2)
            with pe.Fori(1, (STEPS - 3) // 2) as i:
                for u in range(2):
                    one_step(i * 2 + (1 + u), u, i + 2)
            for u in range(2):
                one_step(STEPS - 2 + u, u, (STEPS - 1) // 2 + 1 if u == 0 else None)
            down(STEPS - 1)


def kernel(x, adj, L0_gnn_W, L0_gnn_b, L0_ffn_gate_w, L0_ffn_w1, L0_ffn_w2, L0_ffn_w3, L0_ffn_sw1, L0_ffn_sw2):
    import numpy as np
    import concourse.bacc as bacc
    from concourse.bass_utils import run_bass_kernel_spmd

    def by_rows(w):
        e, r, n = w.shape
        return w.reshape(e, r // P, P, n).transpose(0, 2, 1, 3).reshape(e, P, -1)

    w1 = by_rows(np.asarray(L0_ffn_w1).transpose(0, 2, 1))
    w3 = by_rows(np.asarray(L0_ffn_w3).transpose(0, 2, 1))
    w2 = by_rows(np.asarray(L0_ffn_w2).transpose(0, 2, 1))
    arrays = {
        "x": np.asarray(x),
        "adj_t": np.asarray(adj).T,
        "gnn_w": np.asarray(L0_gnn_W),
        "gnn_b": np.asarray(L0_gnn_b),
        "gate_t": np.asarray(L0_ffn_gate_w).T,
        "experts": np.concatenate([w1, w3, w2], axis=2),
        "sw1_t": np.asarray(L0_ffn_sw1).T,
        "sw2_t": np.asarray(L0_ffn_sw2).T,
    }
    arrays = {f"in_{k}": np.ascontiguousarray(v) for k, v in arrays.items()}
    nc = bacc.Bacc("TRN2", target_bir_lowering=False, num_devices=1)
    args = [nc.dram_tensor(k, v.shape, mybir.dt.from_np(v.dtype), kind="ExternalInput").ap()
            for k, v in arrays.items()]
    out = nc.dram_tensor("out", np.asarray(x).shape, F32, kind="ExternalOutput").ap()
    gnn_moe(nc, *args, out)
    r = run_bass_kernel_spmd(nc, [arrays], core_ids=[0])
    return r.results[0]["out"]
```
